# Optimizing a Trainium2 kernel written in Bass

```python
import numpy as np
import jax
import jax.numpy as jnp

def _softmax(x, axis=-1):
    return jax.nn.softmax(x, axis=axis)
def _gelu(x):
    return jax.nn.gelu(x, approximate=True)
def _silu(x):
    return jax.nn.silu(x)
def _sigmoid(x):
    return jax.nn.sigmoid(x)
def _layernorm(x, axis=-1, eps=1e-5):
    m = jnp.mean(x, axis=axis, keepdims=True)
    v = jnp.var(x, axis=axis, keepdims=True)
    return (x - m) / jnp.sqrt(v + eps)
def _scatter_add(tgt, idx, src, axis=0):
    return tgt.at[idx].add(src)
def _segment_sum(src, seg, n):
    return jax.ops.segment_sum(src, seg, n)

kernel_name = 'mk_adj_resnorm_d4_adj_512_b93380'

def setup_inputs(seed: int = 0):
    np.random.seed(seed)
    _w = jnp.asarray
    def _rec_inputs():
        import jax
        import jax.numpy as jnp
        _gk = jax.random.key(seed)
        x = -0.0002928 + 1 * jax.random.normal(jax.random.fold_in(_gk, 1), (2708, 512), jnp.float32)
        _w = (1.0 + jnp.arange(2708, dtype=jnp.float32)) ** -0.5
        _w = _w / _w.mean()
        _pij = jnp.clip(0.0014771 * _w[:, None] * _w[None, :], 0.0, 1.0)
        _a = jax.random.uniform(jax.random.fold_in(_gk, 2), (2708, 2708)) < _pij
        _a = jnp.logical_or(_a, jnp.eye(2708, dtype=bool))
        _af = _a.astype(jnp.float32)
        _af = _af * jax.random.uniform(jax.random.fold_in(_gk, 3), (2708, 2708), jnp.float32, 0.05, 1)
        adj = _af
        return x, adj
    x, adj = _rec_inputs()
    def _L0_gnn_setup():
        import jax, jax.numpy as jnp
        import numpy as np
        EPS = 1e-08
        key = jax.random.key(seed)
        k1, k2, k3, k4 = jax.random.split(key, 4)
        N, IN, OUT = (8192, 512, 512)
        x = jax.random.normal(k1, (N, IN), dtype=jnp.float32)
        adj = jax.random.uniform(k2, (N, N), dtype=jnp.float32)
        W = jax.random.normal(k3, (OUT, IN), dtype=jnp.float32) * (1.0 / np.sqrt(IN))
        b = jax.random.normal(k4, (OUT,), dtype=jnp.float32) * 0.01
        return {'x': x, 'adj': adj, 'W': W, 'b': b}
    _L0_gnn_all = _L0_gnn_setup()
    _L0_gnn_in = {k: v for k, v in _L0_gnn_all.items() if k in ('W', 'b', )}
    del _L0_gnn_all

    def _L1_gnn_setup():
        import jax, jax.numpy as jnp
        import numpy as np
        N = 8192
        D = 512
        key = jax.random.key(seed)
        k_h, k_a, k_q, k_k, k_v = jax.random.split(key, 5)
        H = jax.random.normal(k_h, (N, D), dtype=jnp.float32)
        A = jax.random.uniform(k_a, (N, N), dtype=jnp.float32)
        W_Q = jax.random.uniform(k_q, (D, D), dtype=jnp.float32)
        W_K = jax.random.uniform(k_k, (D, D), dtype=jnp.float32)
        W_V = jax.random.uniform(k_v, (D, D), dtype=jnp.float32)
        return {'H': H, 'A': A, 'W_Q': W_Q, 'W_K': W_K, 'W_V': W_V}
    _L1_gnn_all = _L1_gnn_setup()
    _L1_gnn_in = {k: v for k, v in _L1_gnn_all.items() if k in ('W_Q', 'W_K', 'W_V', )}
    del _L1_gnn_all

    def _L2_gnn_setup():
        import jax, jax.numpy as jnp
        import numpy as np
        N = 8192
        D = 512
        key = jax.random.key(seed)
        ks = jax.random.split(key, 6)
        s = 1.0 / np.sqrt(D)
        return {'x': jax.random.normal(ks[0], (N, D), jnp.float32), 'spatial_encoding': jax.random.normal(ks[1], (N, N), jnp.float32), 'edge_encoding': jax.random.normal(ks[2], (N, N), jnp.float32), 'Wq': jax.random.normal(ks[3], (D, D), jnp.float32) * s, 'bq': jnp.zeros((D,), jnp.float32), 'Wk': jax.random.normal(ks[4], (D, D), jnp.float32) * s, 'bk': jnp.zeros((D,), jnp.float32), 'Wv': jax.random.normal(ks[5], (D, D), jnp.float32) * s, 'bv': jnp.zeros((D,), jnp.float32)}
    _L2_gnn_all = _L2_gnn_setup()
    _L2_gnn_in = {k: v for k, v in _L2_gnn_all.items() if k in ('Wq', 'bq', 'Wk', 'bk', 'Wv', 'bv', )}
    del _L2_gnn_all

    def _L3_gnn_setup():
        import jax, jax.numpy as jnp
        import numpy as np
        N = 16384
        D_IN = 512
        D_OUT = 512
        AVG_DEG = 32.0
        key = jax.random.key(seed)
        k1, k2, k3, k4 = jax.random.split(key, 4)
        p = AVG_DEG / N
        adjacency = (jax.random.uniform(k1, (N, N)) < p).astype(jnp.float32)
        adjacency = jnp.maximum(adjacency, adjacency.T)
        node_degree = jnp.sum(adjacency, axis=1, keepdims=True) + 1.0
        x = jax.random.normal(k2, (N, D_IN), dtype=jnp.float32)
        W = jax.random.normal(k3, (D_IN, D_OUT), dtype=jnp.float32) * (1.0 / np.sqrt(D_IN))
        b = jax.random.normal(k4, (D_OUT,), dtype=jnp.float32) * 0.01
        return {'x': x, 'adjacency': adjacency, 'node_degree': node_degree, 'W': W, 'b': b}
    _L3_gnn_all = _L3_gnn_setup()
    _L3_gnn_in = {k: v for k, v in _L3_gnn_all.items() if k in ('W', 'b', )}
    del _L3_gnn_all

    return {
        "x": x,
        "adj": adj,
        "L0_gnn_W": _L0_gnn_in["W"],
        "L0_gnn_b": _L0_gnn_in["b"],
        "L1_gnn_W_Q": _L1_gnn_in["W_Q"],
        "L1_gnn_W_K": _L1_gnn_in["W_K"],
        "L1_gnn_W_V": _L1_gnn_in["W_V"],
        "L2_gnn_Wq": _L2_gnn_in["Wq"],
        "L2_gnn_bq": _L2_gnn_in["bq"],
        "L2_gnn_Wk": _L2_gnn_in["Wk"],
        "L2_gnn_bk": _L2_gnn_in["bk"],
        "L2_gnn_Wv": _L2_gnn_in["Wv"],
        "L2_gnn_bv": _L2_gnn_in["bv"],
        "L3_gnn_W": _L3_gnn_in["W"],
        "L3_gnn_b": _L3_gnn_in["b"],
    }

def reference(x, adj, L0_gnn_W, L0_gnn_b, L1_gnn_W_Q, L1_gnn_W_K, L1_gnn_W_V, L2_gnn_Wq, L2_gnn_bq, L2_gnn_Wk, L2_gnn_bk, L2_gnn_Wv, L2_gnn_bv, L3_gnn_W, L3_gnn_b):
    import jax
    import jax.numpy as jnp
    def _L0_gnn_ref(x, adj, W, b):
        import jax, jax.numpy as jnp
        import numpy as np
        EPS = 1e-08
        deg = adj.sum(axis=1)
        dis = (deg + EPS) ** (-0.5)
        a_norm = dis[:, None] * adj * dis[None, :]
        h = a_norm @ x
        return h @ W.T + b

    def _L1_gnn_ref(H, A, W_Q, W_K, W_V):
        import jax, jax.numpy as jnp
        import numpy as np
        N = 8192
        D = 512
        scale = 1.0 / jnp.sqrt(jnp.asarray(H.shape[1], dtype=H.dtype))
        HQ = H @ W_Q
        HK = H @ W_K
        scores = jnp.einsum('nd,md->nm', HQ, HK)
        scores = scores * A * scale
        attn = jax.nn.softmax(scores, axis=1)
        return attn @ (H @ W_V)

    def _L2_gnn_ref(x, spatial_encoding, edge_encoding, Wq, bq, Wk, bk, Wv, bv):
        import jax, jax.numpy as jnp
        import numpy as np
        N = 8192
        D = 512
        q = x @ Wq.T + bq
        k = x @ Wk.T + bk
        v = x @ Wv.T + bv
        scale = 1.0 / jnp.sqrt(jnp.asarray(q.shape[-1], q.dtype))
        a = q @ k.T * scale + spatial_encoding + edge_encoding
        attn = jax.nn.softmax(a, axis=-1)
        return attn @ v

    def _L3_gnn_ref(x, adjacency, node_degree, W, b):
        import jax, jax.numpy as jnp
        import numpy as np
        N = 16384
        D_IN = 512
        D_OUT = 512
        AVG_DEG = 32.0
        n = adjacency.shape[0]
        a_hat = adjacency + jnp.eye(n, dtype=adjacency.dtype)
        dinv = jax.lax.rsqrt(node_degree)
        a_norm = dinv * a_hat * dinv
        pooled = a_norm @ x + x
        return jax.nn.relu(pooled @ W + b)

    deg = jnp.maximum((adj != 0).astype(jnp.float32).sum(-1), 1.0)
    x = _layernorm(x + _L0_gnn_ref(x, adj, L0_gnn_W, L0_gnn_b), axis=-1)
    x = _layernorm(x + _L1_gnn_ref(x, adj, L1_gnn_W_Q, L1_gnn_W_K, L1_gnn_W_V), axis=-1)
    x = _layernorm(x + _L2_gnn_ref(x, adj, adj, L2_gnn_Wq, L2_gnn_bq, L2_gnn_Wk, L2_gnn_bk, L2_gnn_Wv, L2_gnn_bv), axis=-1)
    x = _layernorm(x + _L3_gnn_ref(x, adj, deg[..., None], L3_gnn_W, L3_gnn_b), axis=-1)
    return x


_drawn_inputs = setup_inputs


def setup_inputs(seed=0):
    import zlib

    import numpy as np

    out = dict(_drawn_inputs(seed))
    spreads = {'L2_gnn_bq': (0.0, 0.589), 'L2_gnn_bk': (0.0, 0.8), 'L2_gnn_bv': (0.0, 0.1)}
    factors = {'L3_gnn_b': 8.0}
    for name, (base, spread) in spreads.items():
        noise = np.random.default_rng([zlib.crc32(name.encode()), seed]).standard_normal(out[name].shape)
        drawn = base * np.exp(spread * noise) if base else spread * noise
        out[name] = jnp.asarray(drawn.astype(out[name].dtype))
    for name, factor in factors.items():
        out[name] = (out[name] * factor).astype(out[name].dtype)
    return out
```

```python
from contextlib import ExitStack

import concourse.bass as bass
from concourse import mybir

F32 = mybir.dt.float32
F16 = mybir.dt.float16
BF16 = mybir.dt.bfloat16
I32 = mybir.dt.int32
ACT = mybir.ActivationFunctionType
ALU = mybir.AluOpType
AX = mybir.AxisListType
RMAX = bass.bass_isa.ReduceOp.max

P = 128
N = 2708
D = 512
KD = D // P
TILES = -(-N // P)
NP = TILES * P
TAIL = N - (TILES - 1) * P
CHUNKS = -(-N // 512)
RING = 4
HALF = 3
X_BITS, W_TOP, M_TOP, P_BITS = 10, 14, 13, 14
V_SHIFT = 2.0 ** -(9 + X_BITS)
EXP_MASK = 0x7F800000
LN_EPS = 1e-5
DEG_EPS = 1e-8
RSQRT_D = float(D) ** -0.5
FIRST, LAST = 2, TILES - 2


def width(c):
    return min(512, N - 512 * c)


def blocks(g):
    return range(4 * g, min(4 * g + 4, TILES))


def at_least(engine, semaphore, value):
    if not isinstance(value, int) or value > 0:
        engine.wait_ge(semaphore, value)


def over_tiles(engine, body, first=0, end=TILES):
    for t in range(first, FIRST):
        body(t, t % 2)
    with engine.Fori(FIRST, LAST - 1, 2) as t:
        body(t, 0)
        body(t + 1, 1)
    for t in range(LAST, end):
        body(t, t % 2)


def graph_layers(nc, x, adj, w0, b0, wq1, wk1, wv1, wq2, bq2, wk2, bk2, wv2, bv2, w3, b3, out):
    split_dram = nc.dram_tensor("split_weights", [6, P, 2 * KD * D], F16, kind="Internal").ap()
    V0, V1, V2, V3, M1, M2 = range(6)
    LAYERS = range(4)
    is_attention = [False, True, True, False]

    ctx = ExitStack()
    with ctx:
        def sb(name, shape, dt=F32):
            return ctx.enter_context(nc.sbuf_tensor(name, shape, dt))

        def sem(name):
            return ctx.enter_context(nc.semaphore(name))

        xrow = sb("xrow", [P, TILES, D])
        xT = sb("xT", [P, 2, KD, NP], F16)
        v16 = sb("v16", [P, 2, TILES, D], F16)
        arow = sb("arow", [P, 2, NP])
        pT = sb("pT", [P, RING, 2, 512], F16)
        qT = sb("qT", [P, 2, 2, KD, P], F16)
        w16 = sb("w16", [P, 2, KD, D], F16)
        m16 = sb("m16", [P, 2, KD, D], F16)
        junk = sb("junk", [P, N], BF16)
        bias = sb("bias", [P, 3, D])
        ubk = sb("ubk", [P, D])
        y = sb("y", [P, D])
        upd = sb("upd", [P, D])
        x_stage = [y, upd]
        ident = sb("ident", [P, P])
        bcol = sb("bcol", [P, 2, KD])
        bk_wide = sb("bk_wide", [P, KD, P])
        ones = sb("ones", [P, P])
        mhalf = sb("mhalf", [P, TILES])
        amax = sb("amax", [P, 8])
        bound = sb("bound", [P, 8])
        scale = sb("scale", [P, 8])
        inv = sb("inv", [P, 8])
        amax0 = sb("amax0", [P, 3])
        bound0 = sb("bound0", [P, 3])
        scale0 = sb("scale0", [P, 3])
        inv0 = sb("inv0", [P, 3])
        vq = sb("vq", [P, KD + 1])
        deg = sb("deg", [P, TILES])
        rabs = sb("rabs", [P, TILES])
        dis = sb("dis", [P, TILES])
        count = sb("count", [P, TILES])
        invdeg = sb("invdeg", [P, TILES])
        kz = sb("kz", [P, TILES])
        kout = sb("kout", [P, TILES])
        kself = sb("kself", [P, TILES])
        tmp = sb("tmp", [P, TILES])
        const = sb("const", [P, 4])
        rowsum = sb("rowsum", [P, 2])
        negmax = sb("negmax", [P, 2])
        cmax = sb("cmax", [P, 2, CHUNKS])
        tiny = sb("tiny", [P, 8])
        st6 = sb("st6", [P, 6])
        mv = sb("mv", [P, 2])
        vareps = sb("vareps", [P, 1])
        rstd = sb("rstd", [P, 1])

        whole = [xT[:, :, :, :].rearrange("p h k n -> p (h k n)").bitcast(F32),
                 v16[:, :, :, :].rearrange("p h t n -> p (h t n)").bitcast(F32),
                 m16[:, :, :, :].rearrange("p h k n -> p (h k n)").bitcast(F32)]

        def slot(i):
            at = KD * D * (i % 5)
            return whole[i // 5][:, at:at + KD * D]

        def slot3(i):
            return slot(i).rearrange("p (k n) -> p k n", k=KD)

        WQ1, WK1, WQ1T, WK1T, WQ2, WK2, W0, W0T, WV1, WV2, W3 = range(11)
        M1_SLOT, M2_SLOT, WV2T = WQ1, WK1, WQ1T
        final = [W0T, WV1, WV2T, W3, M1_SLOT, M2_SLOT]

        bank = [ctx.enter_context(nc.psum_tensor(f"bank{i}", [P, 512], F32)) for i in range(8)]
        score_bank, turn_bank, out_bank, q_bank = bank[0:3], bank[3:5], bank[5:7], bank[7]

        w_in = [sem(f"w_in{i}") for i in range(11)]
        small_in = sem("small_in")
        x_in = sem("x_in")
        a0_in = [sem(f"a0_in{i}") for i in range(2)]
        pads_zero = sem("pads_zero")
        constants_set = sem("constants_set")
        ident_zero = sem("ident_zero")
        ident_set = sem("ident_set")
        job_done = sem("job_done")
        job_taken = sem("job_taken")
        bounds_set = sem("bounds_set")
        bounds_all = sem("bounds_all")
        dve_step = sem("dve_step")
        scales_set = sem("scales_set")
        split_hi = sem("split_hi")
        split_lo = sem("split_lo")
        split_stored = sem("split_stored")
        summed_abs = sem("summed_abs")
        summed = sem("summed")
        pow_wanted = sem("pow_wanted")
        pow_done = sem("pow_done")
        phase_done = sem("phase_done")
        out_stored = sem("out_stored")
        w16_in = [None] + [sem(f"L{l}_w16_in") for l in (1, 2, 3)]
        m16_in = [None] + [sem(f"L{l}_m16_in") for l in (1, 2)]

        class Layer:
            def __init__(self, l):
                def named(what):
                    return sem(f"L{l}_{what}")
                self.x_staged = named("x_staged")
                self.x_turned = named("x_turned")
                self.xT_hi = named("xT_hi")
                self.xT_lo = named("xT_lo")
                self.v_ready = named("v_ready")
                self.v_hi = named("v_hi")
                self.v_lo = named("v_lo")
                self.a_in = [[named(f"a_in{s}{h}") for h in range(2)] for s in range(2)]
                self.group_turned = named("group_turned")
                self.group_hi = named("group_hi")
                self.group_lo = named("group_lo")
                self.group_used = named("group_used")
                self.out_taken = named("out_taken")
                self.norm_step = named("norm_step")
                self.var_ready = named("var_ready")
                self.rstd_ready = named("rstd_ready")
                self.row_done = named("row_done")
                if is_attention[l]:
                    self.q_ready = named("q_ready")
                    self.q_hi = named("q_hi")
                    self.q_lo = named("q_lo")
                    self.q_step = named("q_step")
                    self.scores_ready = named("scores_ready")
                    self.scores_taken = named("scores_taken")
                    self.max_step = named("max_step")
                    self.rowmax_ready = named("rowmax_ready")
                    self.probs_ready = named("probs_ready")
                if l == 0:
                    self.counted = named("counted")
        L = [Layer(l) for l in LAYERS]

        block = ctx.enter_context(nc.Block())

        def end_phase(engine, phase):
            engine.drain().then_inc(phase_done, 1)
            engine.wait_ge(phase_done, 4 * phase)

        def cols3(ap):
            return ap.rearrange("p (k n) -> p k n", k=KD)

        @block.sync
        def _(sp):
            for i, w in ((WQ1, wq1), (WK1, wk1), (WQ2, wq2), (WK2, wk2), (WV2, wv2), (W0, w0), (WV1, wv1), (W3, w3)):
                sp.dma_start(slot3(i), w.rearrange("(k p) n -> p k n", p=P)).then_inc(w_in[i], 16)
            sp.dma_start(bcol[:, 0, :], bq2.rearrange("(k p) -> p k", p=P), allow_slow_non_contiguous=True).then_inc(small_in, 16)
            sp.dma_start(bcol[:, 1, :], bk2.rearrange("(k p) -> p k", p=P), allow_slow_non_contiguous=True).then_inc(small_in, 16)
            for i, b in enumerate((b0, bv2, b3)):
                sp.dma_start(bias[:, i, :], b.partition_broadcast(P)).then_inc(small_in, 16)
            sp.wait_ge(pads_zero, 3)
            sp.dma_start(xrow[:, 0:TILES - 1, :],
                         x[0:N - TAIL, :].rearrange("(t p) n -> p t n", p=P)).then_inc(x_in, 16)
            sp.dma_start(xrow[0:TAIL, TILES - 1, :], x[N - TAIL:N, :]).then_inc(x_in, 16)

            for t in range(2):
                sp.dma_start(arow[:, t, 0:N], adj[t * P:(t + 1) * P, :]).then_inc(a0_in[t], 16)

            def first_row(t):
                return t * P if isinstance(t, int) else sp.snap(t * P)

            def first_pass(t, s):
                row0 = first_row(t)
                at_least(sp, summed_abs, t - 1)
                at_least(sp, summed, t - 1)
                if isinstance(t, int) and t == TILES - 1:
                    sp.dma_start(arow[0:TAIL, s, 0:N], adj[N - TAIL:N, :]).then_inc(a0_in[s], 16)
                else:
                    sp.dma_start(arow[:, s, 0:N], adj[bass.ds(row0, P), :]).then_inc(a0_in[s], 16)

            for n, which in enumerate((M1, M2, V1, V2, V3)):
                sp.wait_ge(split_lo, n + 1)
                sp.dma_start(split_dram[which], w16[:, :, :, :].rearrange("p h k n -> p (h k n)"))\
                    .then_inc(split_stored, 16)
            over_tiles(sp, first_pass, first=FIRST)

            for l in LAYERS:
                def load(t, s, l=l):
                    me = L[l]
                    rows = TAIL if isinstance(t, int) and t == TILES - 1 else P
                    row0 = first_row(t)
                    for h, (c0, c1) in enumerate(((0, 512 * HALF), (512 * HALF, N))):
                        if isinstance(t, int) and t < 2:
                            if l == 0:
                                sp.wait_ge(summed_abs, TILES - 1 + t)
                                sp.wait_ge(summed, TILES - 1 + t)
                            else:
                                sp.wait_ge(L[l - 1].group_turned, CHUNKS * (TILES - 2 + t) + (HALF, CHUNKS)[h])
                            if l == 1:
                                sp.wait_ge(L[0].counted, TILES - 1 + t)
                        else:
                            if l == 0:
                                sp.wait_ge(me.group_lo, (t - 1) * CHUNKS)
                            else:
                                sp.wait_ge(me.group_turned, (t - 2) * CHUNKS + (HALF, CHUNKS)[h])
                        sp.dma_start(arow[0:rows, s, c0:c1], adj[bass.ds(row0, rows), c0:c1])\
                            .then_inc(me.a_in[s][h], 16)

                def store(t):
                    rows = TAIL if isinstance(t, int) and t == TILES - 1 else P
                    row0 = first_row(t)
                    sp.wait_ge(L[3].row_done, t + 1)
                    if isinstance(t, int):
                        sp.dma_start(out[t * P:t * P + rows, :], xrow[0:rows, t, :]).then_inc(out_stored, 16)
                    else:
                        sp.dma_start(out[bass.ds(row0, P), :],
                                     xrow[:, bass.ds(t, 1), :].rearrange("p a n -> p (a n)"))\
                            .then_inc(out_stored, 16)

                load(0, 0)
                load(1, 1)
                if l < 3:
                    sp.wait_ge(phase_done, 4 * (2 + 2 * l))
                    sp.dma_start(w16[:, :, :, :].rearrange("p h k n -> p (h k n)"), split_dram[V0 + l + 1])\
                        .then_inc(w16_in[l + 1], 16)
                    over_tiles(sp, load, first=FIRST)
                    if is_attention[l + 1]:
                        sp.wait_ge(phase_done, 4 * (3 + 2 * l))
                        sp.dma_start(m16[:, :, :, :].rearrange("p h k n -> p (h k n)"), split_dram[M1 + l])\
                            .then_inc(m16_in[l + 1], 16)
                else:
                    for t in range(2, 4):
                        load(t, t % 2)
                    with sp.Fori(4, LAST - 1, 2) as t:
                        for j in range(2):
                            load(t + j, j)
                            store(t + (j - 4))
                    for t in range(LAST, TILES):
                        load(t, t % 2)
                    for t in range(LAST - 4, TILES):
                        store(t)
            sp.wait_ge(out_stored, 16 * TILES)

        @block.gpsimd
        def _(pool):
            nc.gpsimd.memset(ident[:, :], 0.0).then_inc(ident_zero, 1)
            pool.wait_ge(ident_zero, 1)
            nc.gpsimd.affine_select(out=ident[:, :], in_=ident[:, :], compare_op=ALU.not_equal, fill=1.0,
                                    base=0, pattern=[[-1, P]], channel_multiplier=1).then_inc(ident_set, 1)
            nc.gpsimd.memset(mhalf[:, :], -0.5).then_inc(constants_set, 1)
            nc.gpsimd.memset(ones[:, :], 1.0).then_inc(constants_set, 1)
            pool.wait_ge(bounds_set, 1)
            nc.gpsimd.partition_all_reduce(bound[:, 0:7], amax[:, 0:7], P, RMAX).then_inc(bounds_all, 1)
            pool.wait_ge(constants_set, 1)
            pool.wait_ge(pow_wanted, 1)
            nc.gpsimd.tensor_tensor(dis[:, :], tmp[:, :], mhalf[:, :], ALU.pow).then_inc(pow_done, 1)
            pool.wait_ge(bounds_set, 2)
            nc.gpsimd.partition_all_reduce(bound0[:, :], amax0[:, :], P, RMAX).then_inc(bounds_all, 1)
            end_phase(pool, 1)
            for l in LAYERS:
                def stage(t, s):
                    at_least(pool, L[l].x_turned, t - 1)
                    nc.gpsimd.tensor_copy(x_stage[s][:, :], xrow[:, bass.ds(t, 1), :].rearrange("p a n -> p (a n)"))\
                        .then_inc(L[l].x_staged, 1)

                over_tiles(pool, stage)
                end_phase(pool, 2 + 2 * l)
                with pool.Fori(0, TILES) as t:
                    pool.wait_ge(L[l].var_ready, t + 1)
                    nc.gpsimd.tensor_tensor(rstd[:, :], vareps[:, :], mhalf[:, 0:1], ALU.pow)\
                        .then_inc(L[l].rstd_ready, 1)
                end_phase(pool, 3 + 2 * l)

        @block.tensor
        def _(pe):
            job = [0]

            def begin_job():
                at_least(pe, job_taken, job[0] - 7)
                b = bank[job[0] % 8]
                job[0] += 1
                return b

            def turn_weights(i):
                pe.wait_ge(w_in[i], 16)
                for o in range(KD):
                    b = begin_job()
                    for k in range(KD):
                        last = nc.tensor.transpose(b[:, k * P:(k + 1) * P], slot3(i)[:, k, o * P:(o + 1) * P], ident[:, :])
                    last.then_inc(job_done, 1)

            def product(left, right):
                for i in range(KD):
                    b = begin_job()
                    for k in range(KD):
                        last = nc.tensor.matmul(b[:, :], slot3(left)[:, k, i * P:(i + 1) * P], slot3(right)[:, k, :],
                                                start=(k == 0), stop=(k == KD - 1))
                    last.then_inc(job_done, 1)

            pe.wait_ge(ident_set, 1)
            turn_weights(WQ1)
            turn_weights(WK1)
            pe.wait_ge(job_taken, 8)
            product(WQ1T, WK1T)
            pe.wait_ge(w_in[WQ2], 16)
            pe.wait_ge(w_in[WK2], 16)
            product(WQ2, WK2)
            pe.wait_ge(small_in, 16 * 5)
            pe.wait_ge(dve_step, 1)
            b = begin_job()
            for k in range(KD):
                last = nc.tensor.matmul(b[:, :], bk_wide[:, k, :], slot3(WQ2)[:, k, :], start=(k == 0), stop=(k == KD - 1))
            last.then_inc(job_done, 1)
            b = begin_job()
            for j in range(KD + 1):
                for k in range(KD):
                    left = slot3(WK2)[:, k, j * P:(j + 1) * P] if j < KD else bk_wide[:, k, :]
                    last = nc.tensor.matmul(b[:, j:j + 1], left, bcol[:, 0, k:k + 1], start=(k == 0), stop=(k == KD - 1))
            last.then_inc(job_done, 1)
            turn_weights(WV2)
            turn_weights(W0)
            end_phase(pe, 1)

            for l in LAYERS:
                me = L[l]

                def turn_x(t, s):
                    at_least(pe, me.xT_lo, t - 1)
                    pe.wait_ge(me.x_staged, t + 1)
                    for k in range(KD):
                        last = nc.tensor.transpose(turn_bank[s][:, k * P:(k + 1) * P],
                                                   x_stage[s][:, k * P:(k + 1) * P], ident[:, :])
                    last.then_inc(me.x_turned, 1)

                def project(t, s):
                    if not (isinstance(t, int) and t == TILES - 1):
                        turn_x(t + 1, 1 - s)
                    pe.wait_ge(me.xT_lo, t + 1)
                    at_least(pe, me.v_lo, t - 1)
                    n = 0
                    for xh, wh in ((0, 0), (0, 1), (1, 0)):
                        for k in range(KD):
                            last = nc.tensor.matmul(out_bank[s][:, :], xT[:, xh, k, bass.ds(t * P, P)],
                                                    w16[:, wh, k, :], start=(n == 0), stop=(n == 3 * KD - 1))
                            n += 1
                    last.then_inc(me.v_ready, 1)

                def turn_group(t, s, g):
                    G = t * CHUNKS + g
                    at_least(pe, me.group_lo, G - 1)
                    if is_attention[l]:
                        if g == 0:
                            pe.wait_ge(me.probs_ready, t + 1)
                    elif g in (0, HALF):
                        pe.wait_ge(me.a_in[s][g // HALF], (t - s) * 8 + 16)
                    b = turn_bank[g % 2]
                    for n, k in enumerate(blocks(g)):
                        last = nc.tensor.transpose(b[:, n * P:(n + 1) * P], arow[:, s, k * P:(k + 1) * P], ident[:, :])
                    last.then_inc(me.group_turned, 1)

                def use_group(t, s, g):
                    G = t * CHUNKS + g
                    r = (2 * s + g) % RING
                    if g == 0:
                        at_least(pe, me.out_taken, t - 1)
                    pe.wait_ge(me.group_lo, G + 1)
                    for n, k in enumerate(blocks(g)):
                        for ph, vh in ((0, 0), (0, 1), (1, 0)):
                            last = nc.tensor.matmul(out_bank[s][:, :], pT[:, r, ph, n * P:(n + 1) * P], v16[:, vh, k, :],
                                                    start=(k == 0 and ph + vh == 0), stop=(k == TILES - 1 and ph == 1))
                    last.then_inc(me.group_used, 1)

                def query(t, s):
                    at_least(pe, me.q_lo, t)
                    for j in range(KD):
                        n = 0
                        for mh, xh in ((0, 0), (0, 1), (1, 0)):
                            for k in range(KD):
                                last = nc.tensor.matmul(q_bank[:, j * P:(j + 1) * P], m16[:, mh, k, j * P:(j + 1) * P],
                                                        xT[:, xh, k, bass.ds(t * P, P)], start=(n == 0), stop=(n == 3 * KD - 1))
                                n += 1
                    last.then_inc(me.q_ready, 1)

                def scores(t, s, c):
                    if c == 0:
                        pe.wait_ge(me.q_lo, t + 1)
                    at_least(pe, me.scores_taken, t * CHUNKS + c - 2)
                    n, w = 0, width(c)
                    for qh, xh in ((0, 0), (0, 1), (1, 0)):
                        for k in range(KD):
                            last = nc.tensor.matmul(score_bank[c % 3][:, 0:w], qT[:, s, qh, k, :],
                                                    xT[:, xh, k, 512 * c:512 * c + w], start=(n == 0), stop=(n == 3 * KD - 1))
                            n += 1
                    last.then_inc(me.scores_ready, 1)

                def rows(t, s):
                    last_tile = isinstance(t, int) and t == TILES - 1
                    if is_attention[l]:
                        for c in range(CHUNKS):
                            if not last_tile:
                                if c == CHUNKS - 1:
                                    turn_group(t, s, 0)
                                scores(t + 1, 1 - s, c)
                                if c == 2 and not (isinstance(t, int) and t >= LAST):
                                    query(t + 2, s)
                        if last_tile:
                            turn_group(t, s, 0)
                    for g in range(CHUNKS):
                        if g + 1 < CHUNKS:
                            turn_group(t, s, g + 1)
                        elif not is_attention[l] and not last_tile:
                            turn_group(t + 1, 1 - s, 0)
                        use_group(t, s, g)

                if l:
                    pe.wait_ge(w16_in[l], 16)
                turn_x(0, 0)
                over_tiles(pe, project)
                end_phase(pe, 2 + 2 * l)
                if is_attention[l]:
                    pe.wait_ge(m16_in[l], 16)
                    query(0, 0)
                    query(1, 1)
                    for c in range(CHUNKS):
                        scores(0, 0, c)
                else:
                    turn_group(0, 0, 0)
                over_tiles(pe, rows)
                end_phase(pe, 3 + 2 * l)

        @block.scalar
        def _(act):
            job = [0]

            def take_job(dst, factor=1.0):
                act.wait_ge(job_done, job[0] + 1)
                b = bank[job[0] % 8]
                job[0] += 1
                nc.scalar.activation(dst, b[:, 0:dst.shape[-1]], ACT.Copy, scale=factor).then_inc(job_taken, 1)

            for i in (WQ1T, WK1T):
                for o in range(KD):
                    take_job(slot3(i)[:, o, :])
            for i in (M1_SLOT, M2_SLOT):
                for o in range(KD):
                    take_job(slot3(i)[:, o, :], RSQRT_D)
            take_job(ubk[:, :], RSQRT_D)
            take_job(vq[:, :], RSQRT_D)
            for i in (WV2T, W0T):
                for o in range(KD):
                    take_job(slot3(i)[:, o, :])
            act.wait_ge(scales_set, 1)
            for n, which in enumerate((M1, M2, V1, V2, V3, V0)):
                if n:
                    act.wait_ge(split_stored, 16 * n)
                if which in (V1, V3):
                    act.wait_ge(w_in[final[which]], 16)
                nc.scalar.activation(w16[:, 0, :, :].rearrange("p k n -> p (k n)"), slot(final[which]), ACT.Copy,
                                     scale=scale[:, which:which + 1]).then_inc(split_hi, 1)

            def sum_abs(t, s):
                act.wait_ge(a0_in[s], (t - s) * 8 + 16)
                at_least(act, summed_abs, t)
                nc.scalar.activation(junk[:, :], arow[:, s, 0:N], ACT.Abs,
                                     accum_out=rabs[:, t:t + 1] if isinstance(t, int) else rabs[:, bass.ds(t, 1)])\
                    .then_inc(summed_abs, 1)

            over_tiles(act, sum_abs)
            end_phase(act, 1)

            for l in LAYERS:
                me = L[l]
                x_factor = scale0[:, 2:3] if l == 0 else 2.0 ** X_BITS

                def project(t, s):
                    act.wait_ge(me.x_turned, t + 1)
                    nc.scalar.activation(xT[:, 0, :, bass.ds(t * P, P)], cols3(turn_bank[s][:, :]), ACT.Copy,
                                         scale=x_factor).then_inc(me.xT_hi, 1)
                    act.wait_ge(me.v_ready, t + 1)
                    factor = kz[:, bass.ds(t, 1)] if l == 0 else V_SHIFT
                    nc.scalar.activation(v16[:, 0, bass.ds(t, 1), :].rearrange("p a n -> p (a n)"), out_bank[s][:, :],
                                         ACT.Copy, scale=factor).then_inc(me.v_hi, 1)

                def group_hi(t, s, g):
                    G = t * CHUNKS + g
                    r = (2 * s + g) % RING
                    act.wait_ge(me.group_turned, G + 1)
                    at_least(act, me.group_used, G - RING + 1)
                    w = P * len(blocks(g))
                    nc.scalar.activation(pT[:, r, 0, 0:w], turn_bank[g % 2][:, 0:w], ACT.Copy,
                                         scale=2.0 ** P_BITS if is_attention[l] else scale0[:, 1:2])\
                        .then_inc(me.group_hi, 1)

                def query_hi(t, s):
                    act.wait_ge(me.q_ready, t + 1)
                    at_least(act, me.scores_ready, (t - 1) * CHUNKS)
                    for j in range(KD):
                        if l == 2:
                            last = nc.scalar.activation(qT[:, s, 0, j, :], q_bank[:, j * P:(j + 1) * P], ACT.Identity,
                                                        scale=V_SHIFT, bias=vq[:, j:j + 1])
                        elif j == 0:
                            last = nc.scalar.activation(qT[:, s, 0, :, :], cols3(q_bank[:, :]), ACT.Copy, scale=V_SHIFT)
                    last.then_inc(me.q_hi, 1)

                def exps(t, s):
                    act.wait_ge(me.rowmax_ready, t + 1)
                    at_least(act, me.out_taken, t - 1)
                    nc.scalar.activation(arow[:, s, 0:N], arow[:, s, 0:N], ACT.Exp, bias=negmax[:, s:s + 1],
                                         scale=const[:, 0:1], accum_out=rowsum[:, s:s + 1]).then_inc(me.probs_ready, 1)

                def rows(t, s):
                    last_tile = isinstance(t, int) and t == TILES - 1
                    if is_attention[l] and not (isinstance(t, int) and t >= LAST):
                        query_hi(t + 2, s)
                    for g in range(CHUNKS):
                        group_hi(t, s, g)
                    if is_attention[l] and not last_tile:
                        exps(t + 1, 1 - s)

                over_tiles(act, project)
                end_phase(act, 2 + 2 * l)
                if is_attention[l]:
                    query_hi(0, 0)
                    query_hi(1, 1)
                    exps(0, 0)
                over_tiles(act, rows)
                end_phase(act, 3 + 2 * l)

        @block.vector
        def _(dve):
            steps = [0]

            def step(ins):
                ins.then_inc(dve_step, 1)
                steps[0] += 1
                dve.wait_ge(dve_step, steps[0])

            def powers(bound_, scale_, inv_, tops):
                w = len(tops)
                step(nc.vector.tensor_scalar(inv_[:, 0:w], bound_[:, 0:w], 2.0 ** -100, 2.0 ** 100, ALU.max, ALU.min))
                step(nc.vector.tensor_scalar(inv_[:, 0:w].bitcast(I32), inv_[:, 0:w].bitcast(I32), EXP_MASK, None,
                                             ALU.bitwise_and))
                step(nc.vector.reciprocal(scale_[:, 0:w], inv_[:, 0:w]))
                for i, top in enumerate(tops):
                    if top:
                        nc.vector.tensor_scalar(scale_[:, i:i + 1], scale_[:, i:i + 1], 2.0 ** top, None, ALU.mult)
                        step(nc.vector.tensor_scalar(inv_[:, i:i + 1], inv_[:, i:i + 1], 2.0 ** -top, None, ALU.mult))

            dve.wait_ge(small_in, 16 * 5)
            dve.wait_ge(constants_set, 2)
            for k in range(KD):
                last = nc.vector.tensor_scalar(bk_wide[:, k, :], ones[:, :], bcol[:, 1, k:k + 1], None, ALU.mult)
            step(last)
            nc.vector.memset(xrow[:, TILES - 1, :], 0.0).then_inc(pads_zero, 1)
            for s in range(2):
                nc.vector.memset(arow[:, s, N:NP], 0.0).then_inc(pads_zero, 1)
            for i, w in ((V0, W0), (V1, WV1), (V2, WV2), (V3, W3)):
                dve.wait_ge(w_in[w], 16)
                nc.vector.tensor_reduce(amax[:, i:i + 1], slot(w), AX.X, ALU.max, apply_absolute_value=True)
            for i, n in ((M1, 12), (M2, 16)):
                dve.wait_ge(job_taken, n)
                nc.vector.tensor_reduce(amax[:, i:i + 1], slot(final[i]), AX.X, ALU.max, apply_absolute_value=True)
            dve.wait_ge(job_taken, 18)
            step(nc.vector.tensor_reduce(amax[:, 6:7], vq[:, 0:KD], AX.X, ALU.max, apply_absolute_value=True))
            nc.vector.tensor_scalar(amax[:, 6:7], amax[:, 6:7], 2.0 ** -9, None, ALU.mult).then_inc(bounds_set, 1)
            dve.wait_ge(bounds_all, 1)
            step(nc.vector.tensor_tensor(bound[:, M2:M2 + 1], bound[:, M2:M2 + 1], bound[:, 6:7], ALU.max))
            powers(bound, scale, inv, [W_TOP] * 4 + [M_TOP] * 2)
            nc.vector.tensor_scalar(vq[:, 0:KD], vq[:, 0:KD], scale[:, M2:M2 + 1], 2.0 ** -9, ALU.mult, ALU.mult)\
                .then_inc(scales_set, 1)
            dve.wait_ge(job_taken, 26)
            for n, which in enumerate((M1, M2, V1, V2, V3, V0)):
                dve.wait_ge(split_hi, n + 1)
                nc.vector.scalar_tensor_tensor(w16[:, 1, :, :].rearrange("p k n -> p (k n)"), slot(final[which]),
                                               scale[:, which:which + 1],
                                               w16[:, 0, :, :].rearrange("p k n -> p (k n)"),
                                               ALU.mult, ALU.subtract).then_inc(split_lo, 1)
            dve.wait_ge(x_in, 32)
            nc.vector.tensor_reduce(amax0[:, 2:3], xrow[:, :, :].rearrange("p t n -> p (t n)"), AX.X, ALU.max,
                                    apply_absolute_value=True)

            def sum_row(t, s):
                dve.wait_ge(a0_in[s], (t - s) * 8 + 16)
                nc.vector.tensor_reduce(deg[:, t:t + 1] if isinstance(t, int) else deg[:, bass.ds(t, 1)],
                                        arow[:, s, 0:N], AX.X, ALU.add).then_inc(summed, 1)

            over_tiles(dve, sum_row)
            dve.wait_ge(summed, TILES)
            nc.vector.tensor_scalar(tmp[:, :], deg[:, :], DEG_EPS, None, ALU.add).then_inc(pow_wanted, 1)
            dve.wait_ge(summed_abs, TILES)
            step(nc.vector.tensor_reduce(amax0[:, 1:2], rabs[:, :], AX.X, ALU.max))
            dve.wait_ge(pow_done, 1)
            nc.vector.tensor_reduce(amax0[:, 0:1], dis[:, :], AX.X, ALU.max).then_inc(bounds_set, 1)
            dve.wait_ge(bounds_all, 2)
            powers(bound0, scale0, inv0, [0, W_TOP, W_TOP])
            step(nc.vector.tensor_scalar(kz[:, :], dis[:, :], scale0[:, 0:1], 2.0 ** -25, ALU.mult, ALU.mult))
            step(nc.vector.tensor_scalar(kout[:, :], dis[:, :], inv0[:, 0:1], inv0[:, 1:2], ALU.mult, ALU.mult))
            step(nc.vector.tensor_scalar(kout[:, :], kout[:, :], inv0[:, 2:3], inv[:, V0:V0 + 1], ALU.mult, ALU.mult))
            step(nc.vector.tensor_scalar(kout[:, :], kout[:, :], 2.0 ** 25, None, ALU.mult))
            end_phase(dve, 1)

            for l in LAYERS:
                me = L[l]
                x_factor = scale0[:, 2:3] if l == 0 else 2.0 ** X_BITS

                def row(buf, t):
                    return buf[:, t, :] if isinstance(t, int) else buf[:, bass.ds(t, 1), :].rearrange("p a n -> p (a n)")

                if is_attention[l]:
                    step(nc.vector.tensor_scalar(const[:, 0:1], inv[:, M1 + l - 1:M1 + l], 0.5, None, ALU.mult))
                    step(nc.vector.tensor_scalar(const[:, 1:2], scale[:, M1 + l - 1:M1 + l], 4.0, None, ALU.mult))
                    step(nc.vector.tensor_scalar(const[:, 2:3], inv[:, V0 + l:V0 + l + 1], 2.0 ** (9 - P_BITS), None, ALU.mult))
                if l == 3:
                    step(nc.vector.tensor_scalar(tmp[:, :], count[:, :], 1.0, None, ALU.max))
                    step(nc.vector.reciprocal(invdeg[:, :], tmp[:, :]))
                    step(nc.vector.tensor_scalar(const[:, 0:1], inv[:, V3:V3 + 1], 2.0 ** 9, None, ALU.mult))
                    step(nc.vector.tensor_scalar(kout[:, :], invdeg[:, :], inv0[:, 1:2], const[:, 0:1], ALU.mult, ALU.mult))
                    step(nc.vector.tensor_scalar(kself[:, :], invdeg[:, :], 1.0, const[:, 0:1], ALU.add, ALU.mult))

                def project(t, s):
                    dve.wait_ge(me.xT_hi, t + 1)
                    nc.vector.scalar_tensor_tensor(xT[:, 1, :, bass.ds(t * P, P)], cols3(turn_bank[s][:, :]), x_factor,
                                                   xT[:, 0, :, bass.ds(t * P, P)], ALU.mult, ALU.subtract)\
                        .then_inc(me.xT_lo, 1)
                    dve.wait_ge(me.v_hi, t + 1)
                    factor = kz[:, bass.ds(t, 1)] if l == 0 else V_SHIFT
                    nc.vector.scalar_tensor_tensor(row(v16[:, 1], t), out_bank[s][:, :], factor, row(v16[:, 0], t),
                                                   ALU.mult, ALU.subtract).then_inc(me.v_lo, 1)

                def group_lo(t, s, g):
                    G = t * CHUNKS + g
                    r = (2 * s + g) % RING
                    dve.wait_ge(me.group_hi, G + 1)
                    w = P * len(blocks(g))
                    nc.vector.scalar_tensor_tensor(pT[:, r, 1, 0:w], turn_bank[g % 2][:, 0:w],
                                                   2.0 ** P_BITS if is_attention[l] else scale0[:, 1:2],
                                                   pT[:, r, 0, 0:w], ALU.mult, ALU.subtract).then_inc(me.group_lo, 1)

                def query_lo(t, s):
                    dve.wait_ge(me.q_hi, t + 1)
                    if l == 2:
                        for j in range(KD):
                            last = nc.vector.tensor_scalar(upd[:, j * P:(j + 1) * P], q_bank[:, j * P:(j + 1) * P], V_SHIFT,
                                                           vq[:, j:j + 1], ALU.mult, ALU.add)
                        last.then_inc(me.q_step, 1)
                        dve.wait_ge(me.q_step, t + 1)
                        nc.vector.tensor_tensor(qT[:, s, 1, :, :], cols3(upd[:, :]), qT[:, s, 0, :, :],
                                                ALU.subtract).then_inc(me.q_lo, 1)
                    else:
                        nc.vector.scalar_tensor_tensor(qT[:, s, 1, :, :], cols3(q_bank[:, :]), V_SHIFT, qT[:, s, 0, :, :],
                                                       ALU.mult, ALU.subtract).then_inc(me.q_lo, 1)

                TILE_STEPS = CHUNKS + (4 if l == 2 else 1)

                def scores_taken(t, s, c):
                    if c in (0, HALF):
                        dve.wait_ge(me.a_in[s][c // HALF], (t - s) * 8 + 16)
                    dve.wait_ge(me.scores_ready, t * CHUNKS + c + 1)
                    a = arow[:, s, 512 * c:512 * c + width(c)]
                    b = score_bank[c % 3][:, 0:width(c)]
                    if l == 1:
                        nc.vector.tensor_tensor(a, b, a, ALU.mult).then_inc(me.scores_taken, 1)
                    else:
                        nc.vector.scalar_tensor_tensor(a, a, const[:, 1:2], b, ALU.mult, ALU.add)\
                            .then_inc(me.scores_taken, 1)

                def chunk_max(t, s, c):
                    dve.wait_ge(me.scores_taken, t * CHUNKS + c + 1)
                    nc.vector.tensor_reduce(cmax[:, s, c:c + 1], arow[:, s, 512 * c:512 * c + width(c)], AX.X, ALU.max)\
                        .then_inc(me.max_step, 1)

                def row_max(t, s):
                    n = t * TILE_STEPS + CHUNKS
                    dve.wait_ge(me.max_step, n)
                    top = tiny[:, 1:2]
                    nc.vector.tensor_reduce(top, cmax[:, s, :], AX.X, ALU.max).then_inc(me.max_step, 1)
                    dve.wait_ge(me.max_step, n + 1)
                    if l == 1:
                        nc.vector.tensor_scalar(negmax[:, s:s + 1], top, const[:, 0:1], -1.0, ALU.mult, ALU.mult)\
                            .then_inc(me.rowmax_ready, 1)
                        return
                    r, r_all, logit_max = tiny[:, 2:3], tiny[:, 3:4], tiny[:, 4:5]
                    nc.vector.scalar_tensor_tensor(junk[:, 0:D], row(xrow, t), 1.0, ubk[:, :], ALU.mult, ALU.mult,
                                                   accum_out=r).then_inc(me.max_step, 1)
                    dve.wait_ge(me.max_step, n + 2)
                    nc.vector.tensor_tensor(r_all, r, vq[:, KD:KD + 1], ALU.add).then_inc(me.max_step, 1)
                    dve.wait_ge(me.max_step, n + 3)
                    nc.vector.tensor_scalar(logit_max, top, const[:, 0:1], r_all, ALU.mult, ALU.add)\
                        .then_inc(me.max_step, 1)
                    dve.wait_ge(me.max_step, n + 4)
                    nc.vector.tensor_tensor(negmax[:, s:s + 1], r_all, logit_max, ALU.subtract)\
                        .then_inc(me.rowmax_ready, 1)

                NORM_STEPS = (2, 3, 4, 4)[l]

                def update(t, s):
                    n = [t * NORM_STEPS]

                    def norm_step(ins):
                        ins.then_inc(me.norm_step, 1)
                        n[0] = n[0] + 1
                        dve.wait_ge(me.norm_step, n[0])

                    acc = out_bank[s][:, :]
                    dve.wait_ge(me.group_used, (t + 1) * CHUNKS)
                    if is_attention[l]:
                        dve.wait_ge(me.probs_ready, t + 1)
                        norm_step(nc.vector.reciprocal(tiny[:, 5:6], rowsum[:, s:s + 1]))
                        norm_step(nc.vector.tensor_tensor(tiny[:, 6:7], tiny[:, 5:6], const[:, 2:3], ALU.mult))
                        nc.vector.scalar_tensor_tensor(y[:, :], acc, tiny[:, 6:7], row(xrow, t), ALU.mult, ALU.add)\
                            .then_inc(me.out_taken, 1)
                        dve.wait_ge(me.out_taken, t + 1)
                        if l == 2:
                            norm_step(nc.vector.tensor_tensor(y[:, :], y[:, :], bias[:, 1, :], ALU.add))
                    elif l == 0:
                        nc.vector.scalar_tensor_tensor(y[:, :], acc, kout[:, bass.ds(t, 1)], row(xrow, t), ALU.mult, ALU.add)\
                            .then_inc(me.out_taken, 1)
                        dve.wait_ge(me.out_taken, t + 1)
                        norm_step(nc.vector.tensor_tensor(y[:, :], y[:, :], bias[:, 0, :], ALU.add))
                    else:
                        norm_step(nc.vector.tensor_tensor(upd[:, :], row(v16[:, 0], t), row(v16[:, 1], t), ALU.add))
                        norm_step(nc.vector.scalar_tensor_tensor(upd[:, :], upd[:, :], kself[:, bass.ds(t, 1)], bias[:, 2, :],
                                                                 ALU.mult, ALU.add))
                        nc.vector.scalar_tensor_tensor(upd[:, :], acc, kout[:, bass.ds(t, 1)], upd[:, :], ALU.mult, ALU.add)\
                            .then_inc(me.out_taken, 1)
                        dve.wait_ge(me.out_taken, t + 1)
                        norm_step(nc.vector.scalar_tensor_tensor(y[:, :], upd[:, :], 0.0, row(xrow, t), ALU.max, ALU.add))
                    nc.vector.bn_stats(st6[:, :], y[:, :])
                    dve.drain()
                    norm_step(nc.vector.bn_aggr(mv[:, :], st6[:, :]))
                    nc.vector.tensor_scalar(vareps[:, :], mv[:, 1:2], LN_EPS, None, ALU.add).then_inc(me.var_ready, 1)

                def normalise(t):
                    dve.wait_ge(me.rstd_ready, t + 1)
                    nc.vector.tensor_scalar(row(xrow, t), y[:, :], mv[:, 0:1], rstd[:, 0:1], ALU.subtract, ALU.mult)\
                        .then_inc(me.row_done, 1)

                def rows(t, s):
                    first = isinstance(t, int) and t == 0
                    last_tile = isinstance(t, int) and t == TILES - 1
                    if is_attention[l]:
                        for c in range(CHUNKS):
                            if not last_tile:
                                scores_taken(t + 1, 1 - s, c)
                                if c == 2 and not (isinstance(t, int) and t >= LAST):
                                    query_lo(t + 2, s)
                                if c:
                                    chunk_max(t + 1, 1 - s, c - 1)
                            if c == 0 and not first:
                                update(t - 1, 1 - s)
                            if c == 3 and not first:
                                normalise(t - 1)
                            if c == 4:
                                group_lo(t, s, 0)
                        if not last_tile:
                            chunk_max(t + 1, 1 - s, CHUNKS - 1)
                            row_max(t + 1, 1 - s)
                        for g in range(1, CHUNKS):
                            group_lo(t, s, g)
                        return
                    for g in range(CHUNKS):
                        group_lo(t, s, g)
                        if g == 1 and not first:
                            update(t - 1, 1 - s)
                        if g == 3 and not first:
                            normalise(t - 1)
                        if l == 0 and g == 4:
                            for h in range(2):
                                dve.wait_ge(me.a_in[s][h], (t - s) * 8 + 16)
                            nc.vector.tensor_scalar(junk[:, :], arow[:, s, 0:N], 0.0, None, ALU.not_equal, ALU.add,
                                                    accum_out=count[:, bass.ds(t, 1)]).then_inc(me.counted, 1)

                over_tiles(dve, project)
                end_phase(dve, 2 + 2 * l)
                if is_attention[l]:
                    query_lo(0, 0)
                    query_lo(1, 1)
                    for c in range(CHUNKS):
                        scores_taken(0, 0, c)
                        chunk_max(0, 0, c)
                    row_max(0, 0)
                over_tiles(dve, rows)
                update(TILES - 1, (TILES - 1) % 2)
                normalise(TILES - 1)
                end_phase(dve, 3 + 2 * l)


_INS = ["x", "adj", "L0_gnn_W", "L0_gnn_b", "L1_gnn_W_Q", "L1_gnn_W_K", "L1_gnn_W_V", "L2_gnn_Wq", "L2_gnn_bq",
        "L2_gnn_Wk", "L2_gnn_bk", "L2_gnn_Wv", "L2_gnn_bv", "L3_gnn_W", "L3_gnn_b"]


def kernel(**inputs):
    import numpy as _np
    import concourse.bacc as _bacc
    from concourse import mybir as _mybir
    from concourse.bass_utils import run_bass_kernel_spmd as _run

    nc = _bacc.Bacc("TRN2", target_bir_lowering=False, num_devices=1)
    arrays, args = {}, []
    for name in _INS:
        a = _np.ascontiguousarray(inputs[name])
        arrays[f"in_{name}"] = a
        args.append(nc.dram_tensor(f"in_{name}", a.shape, _mybir.dt.from_np(a.dtype), kind="ExternalInput").ap())
    args.append(nc.dram_tensor("out_x", (N, D), F32, kind="ExternalOutput").ap())
    graph_layers(nc, *args)
    r = _run(nc, [arrays], core_ids=[0])
    return r.results[0]["out_x"]
```

```python
from contextlib import ExitStack

import concourse.bass as bass
from concourse import mybir

F32 = mybir.dt.float32
F16 = mybir.dt.float16
BF16 = mybir.dt.bfloat16
I32 = mybir.dt.int32
ACT = mybir.ActivationFunctionType
ALU = mybir.AluOpType
AX = mybir.AxisListType
RMAX = bass.bass_isa.ReduceOp.max

P = 128
N = 2708
D = 512
KD = D // P
TILES = -(-N // P)
NP = TILES * P
TAIL = N - (TILES - 1) * P
CHUNKS = -(-N // 512)
RING = 4
HALF = 3
X_BITS, W_TOP, M_TOP, P_BITS = 10, 14, 13, 14
Q1_SHIFT = 2.0 ** -24
V_SHIFT = 2.0 ** -(9 + X_BITS)
EXP_MASK = 0x7F800000
LN_EPS = 1e-5
DEG_EPS = 1e-8
RSQRT_D = float(D) ** -0.5
FIRST, LAST = 2, TILES - 2


TAIL_COPIES = (0, 32, 64)
X_LOADS = 1 + len(TAIL_COPIES)


def loaded(t, s):
    return (t - s) * 8 + 16 * (len(TAIL_COPIES) if isinstance(t, int) and t == TILES - 1 else 1)


def width(c):
    return min(512, N - 512 * c)


def blocks(g):
    return range(4 * g, min(4 * g + 4, TILES))


def at_least(engine, semaphore, value):
    if not isinstance(value, int) or value > 0:
        engine.wait_ge(semaphore, value)


def over_tiles(engine, body, first=0, end=TILES):
    for t in range(first, FIRST):
        body(t, t % 2)
    with engine.Fori(FIRST, LAST - 1, 2) as t:
        body(t, 0)
        body(t + 1, 1)
    for t in range(LAST, end):
        body(t, t % 2)


def graph_layers(nc, x, adj, w0, b0, wq1, wk1, wv1, wq2, bq2, wk2, bk2, wv2, bv2, w3, b3, out):
    split_dram = nc.dram_tensor("split_weights", [7, P, 2 * KD * D], F16, kind="Internal").ap()
    V0, V1, V2, V3, Q1, K1, M2 = range(7)
    LAYERS = range(4)
    is_attention = [False, True, True, False]

    ctx = ExitStack()
    with ctx:
        def sb(name, shape, dt=F32):
            return ctx.enter_context(nc.sbuf_tensor(name, shape, dt))

        def sem(name):
            return ctx.enter_context(nc.semaphore(name))

        xrow = sb("xrow", [P, TILES, D])
        xT = sb("xT", [P, 2, KD, NP], F16)
        v16 = sb("v16", [P, 2, TILES, D], F16)
        arow = sb("arow", [P, 2, NP])
        pT = sb("pT", [P, RING, 2, 512], F16)
        qT = sb("qT", [P, 2, 2, KD, P], F16)
        w16 = sb("w16", [P, 2, KD, D], F16)
        m16 = sb("m16", [P, 2, 2, KD, D], F16)
        junk = m16[:, 1, :, :, :].rearrange("p h k n -> p (h k n)").bitcast(BF16)[:, 0:N]
        q1T = sb("q1T", [P, 2, KD, P], F16)
        bias = sb("bias", [P, 3, D])
        ubk = sb("ubk", [P, D])
        y = sb("y", [P, D])
        upd = sb("upd", [P, D])
        x_stage = [y, upd]
        ident = sb("ident", [P, P])
        bcol = sb("bcol", [P, 2, KD])
        bk_wide = pT[:, 0, :, :].rearrange("p h n -> p (h n)").bitcast(F32).rearrange("p (k n) -> p k n", k=KD)
        ones = sb("ones", [P, P])
        mhalf = sb("mhalf", [P, TILES])
        amax = sb("amax", [P, 8])
        bound = sb("bound", [P, 8])
        scale = sb("scale", [P, 8])
        inv = sb("inv", [P, 8])
        amax0 = sb("amax0", [P, 3])
        bound0 = sb("bound0", [P, 3])
        scale0 = sb("scale0", [P, 3])
        inv0 = sb("inv0", [P, 3])
        vq = sb("vq", [P, KD + 1])
        deg = sb("deg", [P, TILES])
        rabs = sb("rabs", [P, TILES])
        dis = sb("dis", [P, TILES])
        count = sb("count", [P, TILES])
        invdeg = sb("invdeg", [P, TILES])
        kz = sb("kz", [P, TILES])
        kout = sb("kout", [P, TILES])
        kself = sb("kself", [P, TILES])
        tmp = sb("tmp", [P, TILES])
        const = sb("const", [P, 4])
        rowsum = sb("rowsum", [P, 2])
        negmax = sb("negmax", [P, 2])
        cmax = sb("cmax", [P, 2, CHUNKS])
        tiny = sb("tiny", [P, 8])
        st6 = sb("st6", [P, 6])
        mv = sb("mv", [P, 2])
        vareps = sb("vareps", [P, 1])
        rstd = sb("rstd", [P, 1])

        whole = [xT[:, :, :, :].rearrange("p h k n -> p (h k n)").bitcast(F32),
                 v16[:, :, :, :].rearrange("p h t n -> p (h t n)").bitcast(F32),
                 m16[:, 0, :, :, :].rearrange("p h k n -> p (h k n)").bitcast(F32)]

        SPLIT_ORDER = (K1, M2, Q1, V1, V2, V3, V0)
        TILES_AHEAD = 6
        TILES_UNROLLED = TILES_AHEAD + 2 * len(SPLIT_ORDER)

        def slot(i):
            at = KD * D * (i % 5)
            return whole[i // 5][:, at:at + KD * D]

        def slot3(i):
            return slot(i).rearrange("p (k n) -> p k n", k=KD)

        WQ1, WK1, WV2T, WK1T, WQ2, WK2, W0, W0T, WV1, WV2, W3 = range(11)
        M2_SLOT = WK1
        final = [W0T, WV1, WV2T, W3, WQ1, WK1T, M2_SLOT]

        bank = [ctx.enter_context(nc.psum_tensor(f"bank{i}", [P, 512], F32)) for i in range(8)]
        score_bank, turn_bank, out_bank, q_bank = bank[0:3], bank[3:5], bank[5:7], bank[7]

        w_in = [sem(f"w_in{i}") for i in range(11)]
        small_in = sem("small_in")
        x_in = sem("x_in")
        a0_in = [sem(f"a0_in{i}") for i in range(2)]
        pads_zero = sem("pads_zero")
        constants_set = sem("constants_set")
        ident_zero = sem("ident_zero")
        ident_set = sem("ident_set")
        job_done = sem("job_done")
        job_taken = sem("job_taken")
        bounds_set = sem("bounds_set")
        bounds_all = sem("bounds_all")
        dve_step = sem("dve_step")
        scales_set = sem("scales_set")
        tail_split = sem("tail_split")
        split_hi = sem("split_hi")
        split_lo = sem("split_lo")
        split_stored = sem("split_stored")
        summed_abs = sem("summed_abs")
        summed = sem("summed")
        pow_wanted = sem("pow_wanted")
        pow_done = sem("pow_done")
        phase_done = sem("phase_done")
        out_stored = sem("out_stored")
        w16_in = [None] + [sem(f"L{l}_w16_in") for l in (1, 2, 3)]
        m16_in = [None] + [sem(f"L{l}_m16_in") for l in (1, 2)]
        parts_in_m16 = [None, (Q1, K1), (M2,)]

        class Layer:
            def __init__(self, l):
                def named(what):
                    return sem(f"L{l}_{what}")
                self.x_staged = named("x_staged")
                self.x_turned = named("x_turned")
                self.xT_hi = named("xT_hi")
                self.xT_lo = named("xT_lo")
                self.v_ready = named("v_ready")
                self.v_hi = named("v_hi")
                self.v_lo = named("v_lo")
                self.a_in = [[named(f"a_in{s}{h}") for h in range(2)] for s in range(2)]
                self.group_turned = named("group_turned")
                self.group_hi = named("group_hi")
                self.group_lo = named("group_lo")
                self.group_used = named("group_used")
                self.out_taken = named("out_taken")
                self.norm_step = named("norm_step")
                self.var_ready = named("var_ready")
                self.rstd_ready = named("rstd_ready")
                self.row_done = named("row_done")
                if is_attention[l]:
                    self.q_ready = named("q_ready")
                    self.q1_ready = named("q1_ready")
                    self.q1_hi = named("q1_hi")
                    self.q1_lo = named("q1_lo")
                    self.q_hi = named("q_hi")
                    self.q_lo = named("q_lo")
                    self.q_step = named("q_step")
                    self.scores_ready = named("scores_ready")
                    self.scores_taken = named("scores_taken")
                    self.max_step = named("max_step")
                    self.rowmax_ready = named("rowmax_ready")
                    self.exps_done = named("exps_done")
                    self.probs_ready = named("probs_ready")
                else:
                    self.tail_copied = named("tail_copied")
                if l == 0:
                    self.counted = named("counted")
        L = [Layer(l) for l in LAYERS]

        block = ctx.enter_context(nc.Block())

        def end_phase(engine, phase):
            engine.drain().then_inc(phase_done, 1)
            engine.wait_ge(phase_done, 4 * phase)

        tail_start = (TILES - 1) * P

        def copy_tail_columns(s):
            return nc.scalar.activation(
                arow[:, s, tail_start + 32:tail_start + 96].rearrange("p (c n) -> p c n", c=2)[:, :, 0:TAIL],
                arow[:, s:s + 1, tail_start:N].broadcast_to([P, 2, TAIL]), ACT.Copy)

        def cols3(ap):
            return ap.rearrange("p (k n) -> p k n", k=KD)

        @block.sync
        def _(sp):
            sp.dma_start(bcol[:, 0, :], bq2.rearrange("(k p) -> p k", p=P), allow_slow_non_contiguous=True).then_inc(small_in, 16)
            sp.dma_start(bcol[:, 1, :], bk2.rearrange("(k p) -> p k", p=P), allow_slow_non_contiguous=True).then_inc(small_in, 16)
            for i, b in enumerate((b0, bv2, b3)):
                sp.dma_start(bias[:, i, :], b.partition_broadcast(P)).then_inc(small_in, 16)
            for i, w in ((WK1, wk1), (WQ2, wq2), (WK2, wk2), (WV2, wv2), (W0, w0), (WQ1, wq1), (WV1, wv1), (W3, w3)):
                sp.dma_start(slot3(i), w.rearrange("(k p) n -> p k n", p=P)).then_inc(w_in[i], 16)
            sp.wait_ge(pads_zero, 3)
            sp.dma_start(xrow[:, 0:TILES - 1, :],
                         x[0:N - TAIL, :].rearrange("(t p) n -> p t n", p=P)).then_inc(x_in, 16)
            for p0 in TAIL_COPIES:
                sp.dma_start(xrow[p0:p0 + TAIL, TILES - 1, :], x[N - TAIL:N, :]).then_inc(x_in, 16)

            for t in range(2):
                sp.dma_start(arow[:, t, 0:N], adj[t * P:(t + 1) * P, :]).then_inc(a0_in[t], 16)

            def first_row(t):
                return t * P if isinstance(t, int) else sp.snap(t * P)

            def first_pass(t, s):
                row0 = first_row(t)
                at_least(sp, summed_abs, t - 1)
                at_least(sp, summed, t - 1)
                if isinstance(t, int) and t == TILES - 1:
                    for p0 in TAIL_COPIES:
                        sp.dma_start(arow[p0:p0 + TAIL, s, 0:N], adj[N - TAIL:N, :]).then_inc(a0_in[s], 16)
                else:
                    sp.dma_start(arow[:, s, 0:N], adj[bass.ds(row0, P), :]).then_inc(a0_in[s], 16)

            over_tiles(sp, first_pass, first=FIRST)

            for l in LAYERS:
                def load(t, s, l=l):
                    me = L[l]
                    rows = TAIL if isinstance(t, int) and t == TILES - 1 else P
                    row0 = first_row(t)
                    for h, (c0, c1) in enumerate(((0, 512 * HALF), (512 * HALF, N))):
                        if isinstance(t, int) and t < 2:
                            if l == 0:
                                sp.wait_ge(summed_abs, TILES - 1 + t)
                                sp.wait_ge(summed, TILES - 1 + t)
                            else:
                                sp.wait_ge(L[l - 1].group_turned, CHUNKS * (TILES - 2 + t) + (HALF, CHUNKS)[h])
                            if l == 1:
                                sp.wait_ge(L[0].counted, TILES - 1 + t)
                        else:
                            if l == 0:
                                sp.wait_ge(me.group_lo, (t - 1) * CHUNKS)
                            else:
                                sp.wait_ge(me.group_turned, (t - 2) * CHUNKS + (HALF, CHUNKS)[h])
                        for p0 in TAIL_COPIES if rows == TAIL else (0,):
                            sp.dma_start(arow[p0:p0 + rows, s, c0:c1], adj[bass.ds(row0, rows), c0:c1])\
                                .then_inc(me.a_in[s][h], 16)

                def store(t):
                    rows = TAIL if isinstance(t, int) and t == TILES - 1 else P
                    row0 = first_row(t)
                    sp.wait_ge(L[3].row_done, t + 1)
                    if isinstance(t, int):
                        sp.dma_start(out[t * P:t * P + rows, :], xrow[0:rows, t, :]).then_inc(out_stored, 16)
                    else:
                        sp.dma_start(out[bass.ds(row0, P), :],
                                     xrow[:, bass.ds(t, 1), :].rearrange("p a n -> p (a n)"))\
                            .then_inc(out_stored, 16)

                load(0, 0)
                load(1, 1)
                if l < 3:
                    sp.wait_ge(phase_done, 4 * (2 + 2 * l))
                    sp.dma_start(w16[:, :, :, :].rearrange("p h k n -> p (h k n)"), split_dram[V0 + l + 1])\
                        .then_inc(w16_in[l + 1], 16)
                    over_tiles(sp, load, first=FIRST)
                    if is_attention[l + 1]:
                        sp.wait_ge(phase_done, 4 * (3 + 2 * l))
                        for i, part in enumerate(parts_in_m16[l + 1]):
                            sp.dma_start(m16[:, i, :, :, :].rearrange("p h k n -> p (h k n)"), split_dram[part])\
                                .then_inc(m16_in[l + 1], 16)
                else:
                    for t in range(2, 4):
                        load(t, t % 2)
                    with sp.Fori(4, LAST - 1, 2) as t:
                        for j in range(2):
                            load(t + j, j)
                            store(t + (j - 4))
                    for t in range(LAST, TILES):
                        load(t, t % 2)
                    for t in range(LAST - 4, TILES):
                        store(t)
            sp.wait_ge(out_stored, 16 * TILES)

        @block.gpsimd
        def _(pool):
            nc.gpsimd.memset(ident[:, :], 0.0).then_inc(ident_zero, 1)
            pool.wait_ge(ident_zero, 1)
            nc.gpsimd.affine_select(out=ident[:, :], in_=ident[:, :], compare_op=ALU.not_equal, fill=1.0,
                                    base=0, pattern=[[-1, P]], channel_multiplier=1).then_inc(ident_set, 1)
            nc.gpsimd.memset(mhalf[:, :], -0.5).then_inc(constants_set, 1)
            nc.gpsimd.memset(ones[:, :], 1.0).then_inc(constants_set, 1)
            pool.wait_ge(bounds_set, 1)
            nc.gpsimd.partition_all_reduce(bound[:, :], amax[:, :], P, RMAX).then_inc(bounds_all, 1)
            for n, which in enumerate(SPLIT_ORDER[:-1]):
                pool.wait_ge(split_lo, n + 1)
                pool.dma_start(split_dram[which], w16[:, :, :, :].rearrange("p h k n -> p (h k n)"))\
                    .then_inc(split_stored, 16)
            pool.wait_ge(constants_set, 1)
            pool.wait_ge(pow_wanted, 1)
            nc.gpsimd.tensor_tensor(dis[:, :], tmp[:, :], mhalf[:, :], ALU.pow).then_inc(pow_done, 1)
            pool.wait_ge(bounds_set, 2)
            nc.gpsimd.partition_all_reduce(bound0[:, :], amax0[:, :], P, RMAX).then_inc(bounds_all, 1)
            end_phase(pool, 1)
            for l in LAYERS:
                def stage(t, s):
                    at_least(pool, L[l].x_turned, t - 1)
                    nc.gpsimd.tensor_copy(x_stage[s][:, :], xrow[:, bass.ds(t, 1), :].rearrange("p a n -> p (a n)"))\
                        .then_inc(L[l].x_staged, 1)

                over_tiles(pool, stage)
                end_phase(pool, 2 + 2 * l)
                with pool.Fori(0, TILES) as t:
                    pool.wait_ge(L[l].var_ready, t + 1)
                    nc.gpsimd.tensor_tensor(rstd[:, :], vareps[:, :], mhalf[:, 0:1], ALU.pow)\
                        .then_inc(L[l].rstd_ready, 1)
                end_phase(pool, 3 + 2 * l)

        @block.tensor
        def _(pe):
            job = [0]

            def begin_job():
                at_least(pe, job_taken, job[0] - 7)
                b = bank[job[0] % 8]
                job[0] += 1
                return b

            def turn_weights(i):
                pe.wait_ge(w_in[i], 16)
                for o in range(KD):
                    b = begin_job()
                    for k in range(KD):
                        last = nc.tensor.transpose(b[:, k * P:(k + 1) * P], slot3(i)[:, k, o * P:(o + 1) * P], ident[:, :])
                    last.then_inc(job_done, 1)

            def product(left, right):
                for i in range(KD):
                    b = begin_job()
                    for k in range(KD):
                        last = nc.tensor.matmul(b[:, :], slot3(left)[:, k, i * P:(i + 1) * P], slot3(right)[:, k, :],
                                                start=(k == 0), stop=(k == KD - 1))
                    last.then_inc(job_done, 1)

            pe.wait_ge(ident_set, 1)
            turn_weights(WK1)
            pe.wait_ge(w_in[WQ2], 16)
            pe.wait_ge(w_in[WK2], 16)
            product(WQ2, WK2)
            pe.wait_ge(small_in, 16 * 5)
            pe.wait_ge(dve_step, 1)
            b = begin_job()
            for k in range(KD):
                last = nc.tensor.matmul(b[:, :], bk_wide[:, k, :], slot3(WQ2)[:, k, :], start=(k == 0), stop=(k == KD - 1))
            last.then_inc(job_done, 1)
            b = begin_job()
            for j in range(KD + 1):
                for k in range(KD):
                    left = slot3(WK2)[:, k, j * P:(j + 1) * P] if j < KD else bk_wide[:, k, :]
                    last = nc.tensor.matmul(b[:, j:j + 1], left, bcol[:, 0, k:k + 1], start=(k == 0), stop=(k == KD - 1))
            last.then_inc(job_done, 1)
            turn_weights(WV2)
            turn_weights(W0)
            end_phase(pe, 1)

            for l in LAYERS:
                me = L[l]

                def turn_x(t, s):
                    at_least(pe, me.xT_lo, t - 1)
                    pe.wait_ge(me.x_staged, t + 1)
                    for k in range(KD):
                        last = nc.tensor.transpose(turn_bank[s][:, k * P:(k + 1) * P],
                                                   x_stage[s][:, k * P:(k + 1) * P], ident[:, :])
                    last.then_inc(me.x_turned, 1)

                def project(t, s):
                    if not (isinstance(t, int) and t == TILES - 1):
                        turn_x(t + 1, 1 - s)
                    pe.wait_ge(me.xT_lo, t + 1)
                    at_least(pe, me.v_lo, t - 1)
                    n = 0
                    for xh, wh in ((0, 0), (0, 1), (1, 0)):
                        for k in range(KD):
                            last = nc.tensor.matmul(out_bank[s][:, :], xT[:, xh, k, bass.ds(t * P, P)],
                                                    w16[:, wh, k, :], start=(n == 0), stop=(n == 3 * KD - 1))
                            n += 1
                    last.then_inc(me.v_ready, 1)

                def turn_group(t, s, g):
                    G = t * CHUNKS + g
                    at_least(pe, me.group_lo, G - 1)
                    if is_attention[l]:
                        if g == 0:
                            pe.wait_ge(me.probs_ready, t + 1)
                    elif g in (0, HALF):
                        pe.wait_ge(me.a_in[s][g // HALF], loaded(t, s))
                    if g == CHUNKS - 1 and not is_attention[l]:
                        pe.wait_ge(me.tail_copied, t + 1)
                    b = turn_bank[g % 2]
                    for n, k in enumerate(blocks(g)):
                        last = nc.tensor.transpose(b[:, n * P:(n + 1) * P], arow[:, s, k * P:(k + 1) * P], ident[:, :])
                    last.then_inc(me.group_turned, 1)

                def use_group(t, s, g):
                    G = t * CHUNKS + g
                    r = (2 * s + g) % RING
                    if g == 0:
                        at_least(pe, me.out_taken, t - 1)
                    pe.wait_ge(me.group_lo, G + 1)
                    for n, k in enumerate(blocks(g)):
                        for ph, vh in ((0, 0), (0, 1), (1, 0)) if k < TILES - 1 else ((0, 0),):
                            last = nc.tensor.matmul(out_bank[s][:, :], pT[:, r, ph, n * P:(n + 1) * P], v16[:, vh, k, :],
                                                    start=(k == 0 and ph + vh == 0), stop=(k == TILES - 1))
                    last.then_inc(me.group_used, 1)

                def weigh(part, right):
                    for j in range(KD):
                        n = 0
                        for mh, xh in ((0, 0), (0, 1), (1, 0)):
                            for k in range(KD):
                                last = nc.tensor.matmul(q_bank[:, j * P:(j + 1) * P], m16[:, part, mh, k, j * P:(j + 1) * P],
                                                        right(xh, k), start=(n == 0), stop=(n == 3 * KD - 1))
                                n += 1
                    return last

                def first_query(t):
                    at_least(pe, me.q_lo, t)
                    weigh(0, lambda xh, k: xT[:, xh, k, bass.ds(t * P, P)]).then_inc(me.q1_ready, 1)

                def query(t, s):
                    if l == 1:
                        pe.wait_ge(me.q1_lo, t + 1)
                        weigh(1, lambda xh, k: q1T[:, xh, k, :]).then_inc(me.q_ready, 1)
                    else:
                        at_least(pe, me.q_lo, t)
                        weigh(0, lambda xh, k: xT[:, xh, k, bass.ds(t * P, P)]).then_inc(me.q_ready, 1)

                def scores(t, s, c):
                    if c == 0:
                        pe.wait_ge(me.q_lo, t + 1)
                    at_least(pe, me.scores_taken, t * CHUNKS + c - 2)
                    n, w = 0, width(c)
                    for qh, xh in ((0, 0), (0, 1), (1, 0)):
                        for k in range(KD):
                            last = nc.tensor.matmul(score_bank[c % 3][:, 0:w], qT[:, s, qh, k, :],
                                                    xT[:, xh, k, 512 * c:512 * c + w], start=(n == 0), stop=(n == 3 * KD - 1))
                            n += 1
                    last.then_inc(me.scores_ready, 1)

                def rows(t, s):
                    last_tile = isinstance(t, int) and t == TILES - 1
                    if is_attention[l]:
                        for c in range(CHUNKS):
                            if not last_tile:
                                if c == CHUNKS - 1:
                                    turn_group(t, s, 0)
                                scores(t + 1, 1 - s, c)
                                if not (isinstance(t, int) and t >= LAST):
                                    if c == 0 and l == 1:
                                        first_query(t + 2)
                                    if c == 2:
                                        query(t + 2, s)
                        if last_tile:
                            turn_group(t, s, 0)
                    for g in range(CHUNKS):
                        if g + 1 < CHUNKS:
                            turn_group(t, s, g + 1)
                        elif not is_attention[l] and not last_tile:
                            turn_group(t + 1, 1 - s, 0)
                        use_group(t, s, g)

                if l:
                    pe.wait_ge(w16_in[l], 16)
                turn_x(0, 0)
                over_tiles(pe, project)
                end_phase(pe, 2 + 2 * l)
                if is_attention[l]:
                    pe.wait_ge(m16_in[l], 16 * len(parts_in_m16[l]))
                    for t in range(2):
                        if l == 1:
                            first_query(t)
                        query(t, t)
                    for c in range(CHUNKS):
                        scores(0, 0, c)
                else:
                    turn_group(0, 0, 0)
                over_tiles(pe, rows)
                end_phase(pe, 3 + 2 * l)

        @block.scalar
        def _(act):
            job = [0]

            def take_job(dst, factor=1.0):
                act.wait_ge(job_done, job[0] + 1)
                b = bank[job[0] % 8]
                job[0] += 1
                nc.scalar.activation(dst, b[:, 0:dst.shape[-1]], ACT.Copy, scale=factor).then_inc(job_taken, 1)

            for o in range(KD):
                take_job(slot3(WK1T)[:, o, :])
            for o in range(KD):
                take_job(slot3(M2_SLOT)[:, o, :], RSQRT_D)
            take_job(ubk[:, :], RSQRT_D)
            take_job(vq[:, :], RSQRT_D)
            for i in (WV2T, W0T):
                for o in range(KD):
                    take_job(slot3(i)[:, o, :])

            def sum_abs(t, s):
                act.wait_ge(a0_in[s], loaded(t, s))
                at_least(act, summed_abs, t)
                nc.scalar.activation(junk, arow[:, s, 0:N], ACT.Abs,
                                     accum_out=rabs[:, t:t + 1] if isinstance(t, int) else rabs[:, bass.ds(t, 1)])\
                    .then_inc(summed_abs, 1)

            for t in range(TILES_AHEAD):
                sum_abs(t, t % 2)
            act.wait_ge(scales_set, 1)
            for n, which in enumerate(SPLIT_ORDER):
                sum_abs(TILES_AHEAD + 2 * n, 0)
                sum_abs(TILES_AHEAD + 2 * n + 1, 1)
                if n:
                    act.wait_ge(split_stored, 16 * n)
                if which in (V1, V3, Q1):
                    act.wait_ge(w_in[final[which]], 16)
                nc.scalar.activation(w16[:, 0, :, :].rearrange("p k n -> p (k n)"), slot(final[which]), ACT.Copy,
                                     scale=scale[:, which:which + 1]).then_inc(split_hi, 1)
            for t in range(TILES_UNROLLED, TILES):
                sum_abs(t, t % 2)
            end_phase(act, 1)

            for l in LAYERS:
                me = L[l]
                x_factor = scale0[:, 2:3] if l == 0 else 2.0 ** X_BITS

                def turned_hi(t, s):
                    act.wait_ge(me.x_turned, t + 1)
                    nc.scalar.activation(xT[:, 0, :, bass.ds(t * P, P)], cols3(turn_bank[s][:, :]), ACT.Copy,
                                         scale=x_factor).then_inc(me.xT_hi, 1)

                def project(t, s):
                    if not (isinstance(t, int) and t == TILES - 1):
                        turned_hi(t + 1, 1 - s)
                    act.wait_ge(me.v_ready, t + 1)
                    factor = kz[:, bass.ds(t, 1)] if l == 0 else V_SHIFT
                    nc.scalar.activation(v16[:, 0, bass.ds(t, 1), :].rearrange("p a n -> p (a n)"), out_bank[s][:, :],
                                         ACT.Copy, scale=factor).then_inc(me.v_hi, 1)

                def group_hi(t, s, g):
                    G = t * CHUNKS + g
                    r = (2 * s + g) % RING
                    act.wait_ge(me.group_turned, G + 1)
                    at_least(act, me.group_used, G - RING + 1)
                    w = P * len(blocks(g))
                    nc.scalar.activation(pT[:, r, 0, 0:w], turn_bank[g % 2][:, 0:w], ACT.Copy,
                                         scale=2.0 ** P_BITS if is_attention[l] else scale0[:, 1:2])\
                        .then_inc(me.group_hi, 1)

                def query_hi(t, s):
                    act.wait_ge(me.q_ready, t + 1)
                    at_least(act, me.scores_ready, (t - 1) * CHUNKS)
                    for j in range(KD):
                        if l == 2:
                            last = nc.scalar.activation(qT[:, s, 0, j, :], q_bank[:, j * P:(j + 1) * P], ACT.Identity,
                                                        scale=V_SHIFT, bias=vq[:, j:j + 1])
                        elif j == 0:
                            last = nc.scalar.activation(qT[:, s, 0, :, :], cols3(q_bank[:, :]), ACT.Copy, scale=Q1_SHIFT)
                    last.then_inc(me.q_hi, 1)

                def first_query_hi(t):
                    act.wait_ge(me.q1_ready, t + 1)
                    at_least(act, me.q_ready, t)
                    nc.scalar.activation(q1T[:, 0, :, :], cols3(q_bank[:, :]), ACT.Copy, scale=V_SHIFT)\
                        .then_inc(me.q1_hi, 1)

                def exps(t, s):
                    act.wait_ge(me.rowmax_ready, t + 1)
                    at_least(act, me.out_taken, t - 1)
                    nc.scalar.activation(arow[:, s, 0:N], arow[:, s, 0:N], ACT.Exp, bias=negmax[:, s:s + 1],
                                         scale=const[:, 0:1], accum_out=rowsum[:, s:s + 1]).then_inc(me.exps_done, 1)
                    act.wait_ge(me.exps_done, t + 1)
                    copy_tail_columns(s).then_inc(me.probs_ready, 1)

                def rows(t, s):
                    last_tile = isinstance(t, int) and t == TILES - 1
                    if is_attention[l] and not (isinstance(t, int) and t >= LAST):
                        if l == 1:
                            first_query_hi(t + 2)
                        query_hi(t + 2, s)
                    for g in range(CHUNKS):
                        if g == 2 and not is_attention[l]:
                            act.wait_ge(me.a_in[s][1], loaded(t, s))
                            copy_tail_columns(s).then_inc(me.tail_copied, 1)
                        group_hi(t, s, g)
                    if is_attention[l] and not last_tile:
                        exps(t + 1, 1 - s)

                turned_hi(0, 0)
                over_tiles(act, project)
                end_phase(act, 2 + 2 * l)
                if is_attention[l]:
                    for t in range(2):
                        if l == 1:
                            first_query_hi(t)
                        query_hi(t, t)
                    exps(0, 0)
                over_tiles(act, rows)
                end_phase(act, 3 + 2 * l)

        @block.vector
        def _(dve):
            steps = [0]

            def step(ins):
                ins.then_inc(dve_step, 1)
                steps[0] += 1
                dve.wait_ge(dve_step, steps[0])

            def powers(bound_, scale_, inv_, tops):
                w = len(tops)
                step(nc.vector.tensor_scalar(inv_[:, 0:w], bound_[:, 0:w], 2.0 ** -100, 2.0 ** 100, ALU.max, ALU.min))
                step(nc.vector.tensor_scalar(inv_[:, 0:w].bitcast(I32), inv_[:, 0:w].bitcast(I32), EXP_MASK, None,
                                             ALU.bitwise_and))
                step(nc.vector.reciprocal(scale_[:, 0:w], inv_[:, 0:w]))
                for i, top in enumerate(tops):
                    if top:
                        nc.vector.tensor_scalar(scale_[:, i:i + 1], scale_[:, i:i + 1], 2.0 ** top, None, ALU.mult)
                        step(nc.vector.tensor_scalar(inv_[:, i:i + 1], inv_[:, i:i + 1], 2.0 ** -top, None, ALU.mult))

            dve.wait_ge(small_in, 16 * 5)
            dve.wait_ge(constants_set, 2)
            for k in range(KD):
                last = nc.vector.tensor_scalar(bk_wide[:, k, :], ones[:, :], bcol[:, 1, k:k + 1], None, ALU.mult)
            step(last)
            nc.vector.memset(xrow[:, TILES - 1, :], 0.0).then_inc(pads_zero, 1)
            for s in range(2):
                nc.vector.memset(arow[:, s, N:NP], 0.0).then_inc(pads_zero, 1)

            def sum_row(t, s):
                dve.wait_ge(a0_in[s], loaded(t, s))
                nc.vector.tensor_reduce(deg[:, t:t + 1] if isinstance(t, int) else deg[:, bass.ds(t, 1)],
                                        arow[:, s, 0:N], AX.X, ALU.add).then_inc(summed, 1)

            def largest(i, numbers):
                return nc.vector.tensor_reduce(amax[:, i:i + 1], numbers, AX.X, ALU.max, apply_absolute_value=True)

            dve.wait_ge(job_taken, 4)
            largest(K1, slot(WK1T))
            for i, w in ((V2, WV2), (V0, W0), (Q1, WQ1), (V1, WV1), (V3, W3)):
                dve.wait_ge(w_in[w], 16)
                largest(i, slot(w))
            for t in range(TILES_AHEAD - 2):
                sum_row(t, t % 2)
            dve.wait_ge(job_taken, 10)
            largest(M2, slot(M2_SLOT))
            step(largest(7, vq[:, 0:KD]))
            nc.vector.tensor_scalar(amax[:, 7:8], amax[:, 7:8], 2.0 ** -9, None, ALU.mult).then_inc(bounds_set, 1)
            for t in range(TILES_AHEAD - 2, TILES_AHEAD):
                sum_row(t, t % 2)
            dve.wait_ge(x_in, X_LOADS * 16)
            nc.vector.tensor_reduce(amax0[:, 2:3], xrow[:, :, :].rearrange("p t n -> p (t n)"), AX.X, ALU.max,
                                    apply_absolute_value=True)
            dve.wait_ge(bounds_all, 1)
            step(nc.vector.tensor_tensor(bound[:, M2:M2 + 1], bound[:, M2:M2 + 1], bound[:, 7:8], ALU.max))
            powers(bound, scale, inv, [W_TOP] * 6 + [M_TOP])
            nc.vector.tensor_scalar(vq[:, 0:KD], vq[:, 0:KD], scale[:, M2:M2 + 1], 2.0 ** -9, ALU.mult, ALU.mult)\
                .then_inc(scales_set, 1)
            dve.wait_ge(job_taken, 18)
            for n, which in enumerate(SPLIT_ORDER):
                sum_row(TILES_AHEAD + 2 * n, 0)
                sum_row(TILES_AHEAD + 2 * n + 1, 1)
                dve.wait_ge(split_hi, n + 1)
                nc.vector.scalar_tensor_tensor(w16[:, 1, :, :].rearrange("p k n -> p (k n)"), slot(final[which]),
                                               scale[:, which:which + 1],
                                               w16[:, 0, :, :].rearrange("p k n -> p (k n)"),
                                               ALU.mult, ALU.subtract).then_inc(split_lo, 1)
            for t in range(TILES_UNROLLED, TILES):
                sum_row(t, t % 2)
            dve.wait_ge(summed, TILES)
            nc.vector.tensor_scalar(tmp[:, :], deg[:, :], DEG_EPS, None, ALU.add).then_inc(pow_wanted, 1)
            dve.wait_ge(summed_abs, TILES)
            step(nc.vector.tensor_reduce(amax0[:, 1:2], rabs[:, :], AX.X, ALU.max))
            dve.wait_ge(pow_done, 1)
            nc.vector.tensor_reduce(amax0[:, 0:1], dis[:, :], AX.X, ALU.max).then_inc(bounds_set, 1)
            dve.wait_ge(bounds_all, 2)
            powers(bound0, scale0, inv0, [0, W_TOP, W_TOP])
            step(nc.vector.tensor_scalar(kz[:, :], dis[:, :], scale0[:, 0:1], 2.0 ** -25, ALU.mult, ALU.mult))
            step(nc.vector.tensor_scalar(kout[:, :], dis[:, :], inv0[:, 0:1], inv0[:, 1:2], ALU.mult, ALU.mult))
            step(nc.vector.tensor_scalar(kout[:, :], kout[:, :], inv0[:, 2:3], inv[:, V0:V0 + 1], ALU.mult, ALU.mult))
            step(nc.vector.tensor_scalar(kout[:, :], kout[:, :], 2.0 ** 25, None, ALU.mult))
            end_phase(dve, 1)

            for l in LAYERS:
                me = L[l]
                x_factor = scale0[:, 2:3] if l == 0 else 2.0 ** X_BITS

                def row(buf, t):
                    return buf[:, t, :] if isinstance(t, int) else buf[:, bass.ds(t, 1), :].rearrange("p a n -> p (a n)")

                if is_attention[l]:
                    if l == 1:
                        step(nc.vector.tensor_scalar(const[:, 0:1], inv[:, Q1:Q1 + 1], inv[:, K1:K1 + 1], None, ALU.mult))
                        step(nc.vector.tensor_scalar(const[:, 0:1], const[:, 0:1], RSQRT_D * 2.0 ** 23, None, ALU.mult))
                    else:
                        step(nc.vector.tensor_scalar(const[:, 0:1], inv[:, M2:M2 + 1], 0.5, None, ALU.mult))
                        step(nc.vector.tensor_scalar(const[:, 1:2], scale[:, M2:M2 + 1], 4.0, None, ALU.mult))
                    step(nc.vector.tensor_scalar(const[:, 2:3], inv[:, V0 + l:V0 + l + 1], 2.0 ** (9 - P_BITS), None, ALU.mult))
                if l == 3:
                    step(nc.vector.tensor_scalar(tmp[:, :], count[:, :], 1.0, None, ALU.max))
                    step(nc.vector.reciprocal(invdeg[:, :], tmp[:, :]))
                    step(nc.vector.tensor_scalar(const[:, 0:1], inv[:, V3:V3 + 1], 2.0 ** 9, None, ALU.mult))
                    step(nc.vector.tensor_scalar(kout[:, :], invdeg[:, :], inv0[:, 1:2], const[:, 0:1], ALU.mult, ALU.mult))
                    step(nc.vector.tensor_scalar(kself[:, :], invdeg[:, :], 1.0, const[:, 0:1], ALU.add, ALU.mult))

                def turned_lo(t, s):
                    dve.wait_ge(me.xT_hi, t + 1)
                    nc.vector.scalar_tensor_tensor(xT[:, 1, :, bass.ds(t * P, P)], cols3(turn_bank[s][:, :]), x_factor,
                                                   xT[:, 0, :, bass.ds(t * P, P)], ALU.mult, ALU.subtract)\
                        .then_inc(me.xT_lo, 1)

                def project(t, s):
                    if not (isinstance(t, int) and t == TILES - 1):
                        turned_lo(t + 1, 1 - s)
                    dve.wait_ge(me.v_hi, t + 1)
                    factor = kz[:, bass.ds(t, 1)] if l == 0 else V_SHIFT
                    lo = nc.vector.scalar_tensor_tensor(row(v16[:, 1], t), out_bank[s][:, :], factor, row(v16[:, 0], t),
                                                        ALU.mult, ALU.subtract)
                    if isinstance(t, int) and t == TILES - 1:
                        lo.then_inc(tail_split, 1)
                        dve.wait_ge(tail_split, l + 1)
                        second = v16[32:64, 0, t, :]
                        lo = nc.vector.scalar_tensor_tensor(second, out_bank[s][32:64, :],
                                                            kz[32:64, t:t + 1] if l == 0 else V_SHIFT, second,
                                                            ALU.mult, ALU.subtract)
                    lo.then_inc(me.v_lo, 1)

                def group_lo(t, s, g):
                    G = t * CHUNKS + g
                    r = (2 * s + g) % RING
                    dve.wait_ge(me.group_hi, G + 1)
                    w = P * len([k for k in blocks(g) if k < TILES - 1])
                    if g == CHUNKS - 1:
                        third = pT[64:96, r, 0, w:w + P]
                        nc.vector.scalar_tensor_tensor(third, turn_bank[g % 2][64:96, w:w + P],
                                                       2.0 ** P_BITS if is_attention[l] else scale0[64:96, 1:2],
                                                       third, ALU.mult, ALU.subtract)
                    nc.vector.scalar_tensor_tensor(pT[:, r, 1, 0:w], turn_bank[g % 2][:, 0:w],
                                                   2.0 ** P_BITS if is_attention[l] else scale0[:, 1:2],
                                                   pT[:, r, 0, 0:w], ALU.mult, ALU.subtract).then_inc(me.group_lo, 1)

                def query_lo(t, s):
                    dve.wait_ge(me.q_hi, t + 1)
                    if l == 2:
                        for j in range(KD):
                            last = nc.vector.tensor_scalar(upd[:, j * P:(j + 1) * P], q_bank[:, j * P:(j + 1) * P], V_SHIFT,
                                                           vq[:, j:j + 1], ALU.mult, ALU.add)
                        last.then_inc(me.q_step, 1)
                        dve.wait_ge(me.q_step, t + 1)
                        nc.vector.tensor_tensor(qT[:, s, 1, :, :], cols3(upd[:, :]), qT[:, s, 0, :, :],
                                                ALU.subtract).then_inc(me.q_lo, 1)
                    else:
                        nc.vector.scalar_tensor_tensor(qT[:, s, 1, :, :], cols3(q_bank[:, :]), Q1_SHIFT, qT[:, s, 0, :, :],
                                                       ALU.mult, ALU.subtract).then_inc(me.q_lo, 1)

                def first_query_lo(t):
                    dve.wait_ge(me.q1_hi, t + 1)
                    nc.vector.scalar_tensor_tensor(q1T[:, 1, :, :], cols3(q_bank[:, :]), V_SHIFT, q1T[:, 0, :, :],
                                                   ALU.mult, ALU.subtract).then_inc(me.q1_lo, 1)

                TILE_STEPS = CHUNKS + (4 if l == 2 else 1)

                def scores_taken(t, s, c):
                    if c in (0, HALF):
                        dve.wait_ge(me.a_in[s][c // HALF], loaded(t, s))
                    dve.wait_ge(me.scores_ready, t * CHUNKS + c + 1)
                    a = arow[:, s, 512 * c:512 * c + width(c)]
                    b = score_bank[c % 3][:, 0:width(c)]
                    if l == 1:
                        nc.vector.tensor_tensor(a, b, a, ALU.mult).then_inc(me.scores_taken, 1)
                    else:
                        nc.vector.scalar_tensor_tensor(a, a, const[:, 1:2], b, ALU.mult, ALU.add)\
                            .then_inc(me.scores_taken, 1)

                def chunk_max(t, s, c):
                    dve.wait_ge(me.scores_taken, t * CHUNKS + c + 1)
                    nc.vector.tensor_reduce(cmax[:, s, c:c + 1], arow[:, s, 512 * c:512 * c + width(c)], AX.X, ALU.max)\
                        .then_inc(me.max_step, 1)

                def row_max(t, s):
                    n = t * TILE_STEPS + CHUNKS
                    dve.wait_ge(me.max_step, n)
                    top = tiny[:, 1:2]
                    nc.vector.tensor_reduce(top, cmax[:, s, :], AX.X, ALU.max).then_inc(me.max_step, 1)
                    dve.wait_ge(me.max_step, n + 1)
                    if l == 1:
                        nc.vector.tensor_scalar(negmax[:, s:s + 1], top, const[:, 0:1], -1.0, ALU.mult, ALU.mult)\
                            .then_inc(me.rowmax_ready, 1)
                        return
                    r, r_all, logit_max = tiny[:, 2:3], tiny[:, 3:4], tiny[:, 4:5]
                    nc.vector.scalar_tensor_tensor(junk[:, 0:D], row(xrow, t), 1.0, ubk[:, :], ALU.mult, ALU.mult,
                                                   accum_out=r).then_inc(me.max_step, 1)
                    dve.wait_ge(me.max_step, n + 2)
                    nc.vector.tensor_tensor(r_all, r, vq[:, KD:KD + 1], ALU.add).then_inc(me.max_step, 1)
                    dve.wait_ge(me.max_step, n + 3)
                    nc.vector.tensor_scalar(logit_max, top, const[:, 0:1], r_all, ALU.mult, ALU.add)\
                        .then_inc(me.max_step, 1)
                    dve.wait_ge(me.max_step, n + 4)
                    nc.vector.tensor_tensor(negmax[:, s:s + 1], r_all, logit_max, ALU.subtract)\
                        .then_inc(me.rowmax_ready, 1)

                NORM_STEPS = (2, 3, 4, 4)[l]

                def update(t, s):
                    n = [t * NORM_STEPS]

                    def norm_step(ins):
                        ins.then_inc(me.norm_step, 1)
                        n[0] = n[0] + 1
                        dve.wait_ge(me.norm_step, n[0])

                    acc = out_bank[s][:, :]
                    dve.wait_ge(me.group_used, (t + 1) * CHUNKS)
                    if is_attention[l]:
                        dve.wait_ge(me.probs_ready, t + 1)
                        norm_step(nc.vector.reciprocal(tiny[:, 5:6], rowsum[:, s:s + 1]))
                        norm_step(nc.vector.tensor_tensor(tiny[:, 6:7], tiny[:, 5:6], const[:, 2:3], ALU.mult))
                        nc.vector.scalar_tensor_tensor(y[:, :], acc, tiny[:, 6:7], row(xrow, t), ALU.mult, ALU.add)\
                            .then_inc(me.out_taken, 1)
                        dve.wait_ge(me.out_taken, t + 1)
                        if l == 2:
                            norm_step(nc.vector.tensor_tensor(y[:, :], y[:, :], bias[:, 1, :], ALU.add))
                    elif l == 0:
                        nc.vector.scalar_tensor_tensor(y[:, :], acc, kout[:, bass.ds(t, 1)], row(xrow, t), ALU.mult, ALU.add)\
                            .then_inc(me.out_taken, 1)
                        dve.wait_ge(me.out_taken, t + 1)
                        norm_step(nc.vector.tensor_tensor(y[:, :], y[:, :], bias[:, 0, :], ALU.add))
                    else:
                        norm_step(nc.vector.tensor_tensor(upd[:, :], row(v16[:, 0], t), row(v16[:, 1], t), ALU.add))
                        norm_step(nc.vector.scalar_tensor_tensor(upd[:, :], upd[:, :], kself[:, bass.ds(t, 1)], bias[:, 2, :],
                                                                 ALU.mult, ALU.add))
                        nc.vector.scalar_tensor_tensor(upd[:, :], acc, kout[:, bass.ds(t, 1)], upd[:, :], ALU.mult, ALU.add)\
                            .then_inc(me.out_taken, 1)
                        dve.wait_ge(me.out_taken, t + 1)
                        norm_step(nc.vector.scalar_tensor_tensor(y[:, :], upd[:, :], 0.0, row(xrow, t), ALU.max, ALU.add))
                    nc.vector.bn_stats(st6[:, :], y[:, :])
                    dve.drain()
                    norm_step(nc.vector.bn_aggr(mv[:, :], st6[:, :]))
                    nc.vector.tensor_scalar(vareps[:, :], mv[:, 1:2], LN_EPS, None, ALU.add).then_inc(me.var_ready, 1)

                def normalise(t):
                    dve.wait_ge(me.rstd_ready, t + 1)
                    nc.vector.tensor_scalar(row(xrow, t), y[:, :], mv[:, 0:1], rstd[:, 0:1], ALU.subtract, ALU.mult)\
                        .then_inc(me.row_done, 1)

                def rows(t, s):
                    first = isinstance(t, int) and t == 0
                    last_tile = isinstance(t, int) and t == TILES - 1
                    if is_attention[l]:
                        for c in range(CHUNKS):
                            if not last_tile:
                                scores_taken(t + 1, 1 - s, c)
                                if not (isinstance(t, int) and t >= LAST):
                                    if c == 0 and l == 1:
                                        first_query_lo(t + 2)
                                    if c == 2:
                                        query_lo(t + 2, s)
                                if c:
                                    chunk_max(t + 1, 1 - s, c - 1)
                            if c == 0 and not first:
                                update(t - 1, 1 - s)
                            if c == 3 and not first:
                                normalise(t - 1)
                            if c == 4:
                                group_lo(t, s, 0)
                        if not last_tile:
                            chunk_max(t + 1, 1 - s, CHUNKS - 1)
                            row_max(t + 1, 1 - s)
                        for g in range(1, CHUNKS):
                            group_lo(t, s, g)
                        return
                    for g in range(CHUNKS):
                        group_lo(t, s, g)
                        if g == 1 and not first:
                            update(t - 1, 1 - s)
                        if g == 3 and not first:
                            normalise(t - 1)
                        if l == 0 and g == 4:
                            for h in range(2):
                                dve.wait_ge(me.a_in[s][h], loaded(t, s))
                            nc.vector.tensor_scalar(junk, arow[:, s, 0:N], 0.0, None, ALU.not_equal, ALU.add,
                                                    accum_out=count[:, bass.ds(t, 1)]).then_inc(me.counted, 1)

                turned_lo(0, 0)
                over_tiles(dve, project)
                end_phase(dve, 2 + 2 * l)
                if is_attention[l]:
                    for t in range(2):
                        if l == 1:
                            first_query_lo(t)
                        query_lo(t, t)
                    for c in range(CHUNKS):
                        scores_taken(0, 0, c)
                        chunk_max(0, 0, c)
                    row_max(0, 0)
                over_tiles(dve, rows)
                update(TILES - 1, (TILES - 1) % 2)
                normalise(TILES - 1)
                end_phase(dve, 3 + 2 * l)


_INS = ["x", "adj", "L0_gnn_W", "L0_gnn_b", "L1_gnn_W_Q", "L1_gnn_W_K", "L1_gnn_W_V", "L2_gnn_Wq", "L2_gnn_bq",
        "L2_gnn_Wk", "L2_gnn_bk", "L2_gnn_Wv", "L2_gnn_bv", "L3_gnn_W", "L3_gnn_b"]


def kernel(**inputs):
    import numpy as _np
    import concourse.bacc as _bacc
    from concourse import mybir as _mybir
    from concourse.bass_utils import run_bass_kernel_spmd as _run

    nc = _bacc.Bacc("TRN2", target_bir_lowering=False, num_devices=1)
    arrays, args = {}, []
    for name in _INS:
        a = _np.ascontiguousarray(inputs[name])
        arrays[f"in_{name}"] = a
        args.append(nc.dram_tensor(f"in_{name}", a.shape, _mybir.dt.from_np(a.dtype), kind="ExternalInput").ap())
    args.append(nc.dram_tensor("out_x", (N, D), F32, kind="ExternalOutput").ap())
    graph_layers(nc, *args)
    r = _run(nc, [arrays], core_ids=[0])
    return r.results[0]["out_x"]
```

```python
from contextlib import ExitStack

import concourse.bass as bass
from concourse import mybir

F32 = mybir.dt.float32
F16 = mybir.dt.float16
BF16 = mybir.dt.bfloat16
I32 = mybir.dt.int32
ACT = mybir.ActivationFunctionType
ALU = mybir.AluOpType
AX = mybir.AxisListType
RMAX = bass.bass_isa.ReduceOp.max

P = 128
N = 2708
D = 512
KD = D // P
TILES = -(-N // P)
NP = TILES * P
TAIL = N - (TILES - 1) * P
CHUNKS = -(-N // 512)
RING = 4
HALF = 3
X_BITS, W_TOP, M_TOP, P_BITS = 10, 14, 13, 14
Q1_SHIFT = 2.0 ** -24
V_SHIFT = 2.0 ** -(9 + X_BITS)
EXP_MASK = 0x7F800000
LN_EPS = 1e-5
DEG_EPS = 1e-8
RSQRT_D = float(D) ** -0.5
FIRST, LAST = 2, TILES - 2
PRESTAGED = 4

TAIL_COPIES = (0, 32, 64)
X_LOADS = 1 + len(TAIL_COPIES)


def loaded(t, s):
    return (t - s) * 8 + 16 * (len(TAIL_COPIES) if isinstance(t, int) and t == TILES - 1 else 1)


def width(c):
    return min(512, N - 512 * c)


def blocks(g):
    return range(4 * g, min(4 * g + 4, TILES))


def at_least(engine, semaphore, value):
    if not isinstance(value, int) or value > 0:
        engine.wait_ge(semaphore, value)


def over_tiles(engine, body, first=0, end=TILES):
    for t in range(first, FIRST):
        body(t, t % 2)
    with engine.Fori(FIRST, LAST - 1, 2) as t:
        body(t, 0)
        body(t + 1, 1)
    for t in range(LAST, end):
        body(t, t % 2)


def graph_layers(nc, x, adj, w0, b0, wq1, wk1, wv1, wq2, bq2, wk2, bk2, wv2, bv2, w3, b3, out):
    split_dram = nc.dram_tensor("split_weights", [7, P, 2 * KD * D], F16, kind="Internal").ap()
    turned_dram = nc.dram_tensor("turned_adjacency", [TILES, P, 2, NP], F16, kind="Internal").ap()
    V0, V1, V2, V3, Q1, K1, M2 = range(7)
    LAYERS = range(4)
    is_attention = [False, True, True, False]

    ctx = ExitStack()
    with ctx:
        def sb(name, shape, dt=F32):
            return ctx.enter_context(nc.sbuf_tensor(name, shape, dt))

        def sem(name):
            return ctx.enter_context(nc.semaphore(name))

        xrow = sb("xrow", [P, TILES, D])
        xT = sb("xT", [P, 2, KD, NP], F16)
        v16 = sb("v16", [P, TILES, 2, D], F16)
        arow = sb("arow", [P, 2, NP])
        turned = arow[:, :, :].rearrange("p s n -> p (s n)").bitcast(F16).rearrange("p (s h n) -> p s h n", s=2, h=2)
        pT = sb("pT", [P, RING, 2, 512], F16)
        qT = sb("qT", [P, 2, 2, KD, P], F16)
        w16 = sb("w16", [P, 2, KD, D], F16)
        m16 = sb("m16", [P, 2, 2, KD, D], F16)
        junk = m16[:, 1, :, :, :].rearrange("p h k n -> p (h k n)").bitcast(BF16)[:, 0:N]
        q1T = sb("q1T", [P, 2, KD, P], F16)
        bias = sb("bias", [P, 3, D])
        ubk = sb("ubk", [P, D])
        y = sb("y", [P, D])
        upd = sb("upd", [P, D])
        x_stage = [qT[:, s, :, :, :].rearrange("p h k n -> p (h k n)").bitcast(F32) for s in range(2)]
        ident = sb("ident", [P, P])
        bcol = sb("bcol", [P, 2, KD])
        bk_wide = pT[:, 0, :, :].rearrange("p h n -> p (h n)").bitcast(F32).rearrange("p (k n) -> p k n", k=KD)
        ones = sb("ones", [P, P])
        mhalf = sb("mhalf", [P, TILES])
        amax = sb("amax", [P, 8])
        bound = sb("bound", [P, 8])
        scale = sb("scale", [P, 8])
        inv = sb("inv", [P, 8])
        xmax = sb("xmax", [P, 4])
        amax0 = sb("amax0", [P, 3])
        bound0 = sb("bound0", [P, 3])
        scale0 = sb("scale0", [P, 3])
        inv0 = sb("inv0", [P, 3])
        vq = sb("vq", [P, KD + 1])
        deg = sb("deg", [P, TILES])
        rabs = sb("rabs", [P, TILES])
        dis = sb("dis", [P, TILES])
        count = sb("count", [P, TILES])
        invdeg = sb("invdeg", [P, TILES])
        kz = sb("kz", [P, TILES])
        kout = sb("kout", [P, TILES])
        kself = sb("kself", [P, TILES])
        tmp = sb("tmp", [P, TILES])
        const = sb("const", [P, 4])
        rowsum = sb("rowsum", [P, 2])
        negmax = sb("negmax", [P, 2])
        cmax = sb("cmax", [P, 2, CHUNKS])
        tiny = sb("tiny", [P, 8])
        st6 = sb("st6", [P, 6])
        mv = sb("mv", [P, 2])
        vareps = sb("vareps", [P, 1])
        rstd = sb("rstd", [P, 1])

        whole = [xT[:, :, :, :].rearrange("p h k n -> p (h k n)").bitcast(F32),
                 v16[:, :, :, :].rearrange("p t h n -> p (t h n)").bitcast(F32),
                 m16[:, 0, :, :, :].rearrange("p h k n -> p (h k n)").bitcast(F32)]

        SPLIT_ORDER = (K1, M2, Q1, V1, V2, V3, V0)
        split_at = [w16[:, :, :, :].rearrange("p h k n -> p h (k n)"),
                    pT[:, :, :, :].rearrange("p r h n -> p (r h n)").rearrange("p (h n) -> p h n", h=2)]
        SUM_AFTER_SPLIT = (1, 2, 3, 4, 5, 6)
        TILES_SPLIT = 2 + len(SUM_AFTER_SPLIT)
        X_PARTS = 4
        x_part = [range(TILES * i // X_PARTS, TILES * (i + 1) // X_PARTS) for i in range(X_PARTS)]

        def projected_by(t):
            return (t + 1 - TILES_SPLIT) * (TILES - 2) // (TILES - TILES_SPLIT)

        def v_whole(t):
            if t < TILES - 2:
                return v16[:, t + 2, :, :].rearrange("p h n -> p (h n)").bitcast(F32)
            return m16[:, 0, t - (TILES - 2), :, :].rearrange("p k n -> p (k n)").bitcast(F32)[:, 0:D]

        def slot(i):
            at = KD * D * (i % 5)
            return whole[i // 5][:, at:at + KD * D]

        def slot3(i):
            return slot(i).rearrange("p (k n) -> p k n", k=KD)

        WQ1, WK1, WV2T, WK1T, WQ2, WK2, W0, W0T, WV1, WV2, W3 = range(11)
        M2_SLOT = WK1
        final = [W0T, WV1, WV2T, W3, WQ1, WK1T, M2_SLOT]

        bank = [ctx.enter_context(nc.psum_tensor(f"bank{i}", [P, 512], F32)) for i in range(8)]
        score_bank, turn_bank, out_bank, q_bank = bank[0:3], bank[3:5], bank[5:7], bank[7]

        w_in = {i: sem(f"w_in{i}") for i in (WK1, WQ2, WK2, WV2, W0, WQ1, WV1, W3)}
        small_in = sem("small_in")
        x_in = sem("x_in")
        a0_in = [sem(f"a0_in{i}") for i in range(2)]
        pads_zero = sem("pads_zero")
        constants_set = sem("constants_set")
        ident_zero = sem("ident_zero")
        ident_set = sem("ident_set")
        job_done = sem("job_done")
        job_taken = sem("job_taken")
        bounds_set = sem("bounds_set")
        bounds_all = sem("bounds_all")
        dve_step = sem("dve_step")
        scales_set = sem("scales_set")
        tail_split = sem("tail_split")
        group_kept = [sem(f"group_kept{r}") for r in range(RING)]
        split_hi = sem("split_hi")
        split_lo = sem("split_lo")
        split_stored = [sem(f"split_stored{i}") for i in range(2)]
        summed_abs = sem("summed_abs")
        summed = sem("summed")
        pow_wanted = sem("pow_wanted")
        pow_done = sem("pow_done")
        x_scale_set = sem("x_scale_set")
        factors_set = sem("factors_set")
        out_stored = sem("out_stored")
        w16_in = [None] + [sem(f"L{l}_w16_in") for l in (1, 2, 3)]
        m16_in = [None] + [sem(f"L{l}_m16_in") for l in (1, 2)]
        parts_in_m16 = [None, (Q1, K1), (M2,)]

        class Layer:
            def __init__(self, l):
                def named(what):
                    return sem(f"L{l}_{what}")
                self.x_staged = named("x_staged")
                self.x_turned = named("x_turned")
                self.xT_hi = named("xT_hi")
                self.xT_lo = named("xT_lo")
                self.v_ready = named("v_ready")
                self.v_hi = named("v_hi")
                self.v_lo = named("v_lo")
                self.a_in = [[named(f"a_in{s}{h}") for h in range(2)] for s in range(2)]
                self.group_turned = named("group_turned")
                self.group_hi = named("group_hi")
                self.group_lo = named("group_lo")
                self.last_lo = named("last_lo")
                self.group_used = named("group_used")
                self.out_taken = named("out_taken")
                self.norm_step = named("norm_step")
                self.var_ready = named("var_ready")
                self.rstd_ready = named("rstd_ready")
                self.row_done = named("row_done")
                if is_attention[l]:
                    self.q_ready = named("q_ready")
                    self.q_hi = named("q_hi")
                    self.q_lo = named("q_lo")
                    self.q_step = named("q_step")
                    self.scores_ready = named("scores_ready")
                    self.scores_taken = named("scores_taken")
                    self.max_step = named("max_step")
                    self.rowmax_ready = named("rowmax_ready")
                    self.exps_done = named("exps_done")
                    self.probs_ready = named("probs_ready")
                else:
                    self.tail_copied = named("tail_copied")
                if l == 1:
                        self.q1_ready = named("q1_ready")
                        self.q1_hi = named("q1_hi")
                        self.q1_lo = named("q1_lo")
                if l == 0:
                    self.v_kept = named("v_kept")
                    self.counted = named("counted")
        L = [Layer(l) for l in LAYERS]

        block = ctx.enter_context(nc.Block())

        tail_start = (TILES - 1) * P

        def copy_tail_columns(s):
            return nc.scalar.activation(
                arow[:, s, tail_start + 32:tail_start + 96].rearrange("p (c n) -> p c n", c=2)[:, :, 0:TAIL],
                arow[:, s:s + 1, tail_start:N].broadcast_to([P, 2, TAIL]), ACT.Copy)

        def cols3(ap):
            return ap.rearrange("p (k n) -> p k n", k=KD)

        @block.sync
        def _(sp):
            sp.dma_start(bcol[:, 0, :], bq2.rearrange("(k p) -> p k", p=P), allow_slow_non_contiguous=True).then_inc(small_in, 16)
            sp.dma_start(bcol[:, 1, :], bk2.rearrange("(k p) -> p k", p=P), allow_slow_non_contiguous=True).then_inc(small_in, 16)
            for i, b in enumerate((b0, bv2, b3)):
                sp.dma_start(bias[:, i, :], b.partition_broadcast(P)).then_inc(small_in, 16)
            for i, w in ((WK1, wk1), (WQ2, wq2), (WK2, wk2), (WV2, wv2), (W0, w0), (WQ1, wq1), (WV1, wv1), (W3, w3)):
                sp.dma_start(slot3(i), w.rearrange("(k p) n -> p k n", p=P)).then_inc(w_in[i], 16)
            for t in range(2):
                sp.dma_start(arow[:, t, 0:N], adj[t * P:(t + 1) * P, :]).then_inc(a0_in[t], 16)

            sp.wait_ge(pads_zero, 3)
            sp.dma_start(xrow[:, 0:TILES - 1, :],
                         x[0:N - TAIL, :].rearrange("(t p) n -> p t n", p=P)).then_inc(x_in, 16)
            for p0 in TAIL_COPIES:
                sp.dma_start(xrow[p0:p0 + TAIL, TILES - 1, :], x[N - TAIL:N, :]).then_inc(x_in, 16)

            def first_row(t):
                return t * P if isinstance(t, int) else sp.snap(t * P)

            def first_pass(t, s):
                row0 = first_row(t)
                at_least(sp, summed_abs, t - 1)
                at_least(sp, summed, t - 1)
                if isinstance(t, int) and t == TILES - 1:
                    for p0 in TAIL_COPIES:
                        sp.dma_start(arow[p0:p0 + TAIL, s, 0:N], adj[N - TAIL:N, :]).then_inc(a0_in[s], 16)
                else:
                    sp.dma_start(arow[:, s, 0:N], adj[bass.ds(row0, P), :]).then_inc(a0_in[s], 16)

            over_tiles(sp, first_pass, first=FIRST)

            for l in LAYERS:
                def load(t, s, l=l):
                    me = L[l]
                    rows = TAIL if isinstance(t, int) and t == TILES - 1 else P
                    row0 = first_row(t)
                    for h, (c0, c1) in enumerate(((0, 512 * HALF), (512 * HALF, N))):
                        if isinstance(t, int) and t < 2:
                            if l == 0:
                                sp.wait_ge(summed_abs, TILES - 1 + t)
                                sp.wait_ge(summed, TILES - 1 + t)
                            else:
                                sp.wait_ge(L[l - 1].group_turned, CHUNKS * (TILES - 2 + t) + (HALF, CHUNKS)[h])
                            if l == 1:
                                sp.wait_ge(L[0].counted, TILES - 1 + t)
                        else:
                            if l == 0:
                                sp.wait_ge(me.group_lo, (t - 1) * CHUNKS)
                            else:
                                sp.wait_ge(me.group_turned, (t - 2) * CHUNKS + (HALF, CHUNKS)[h])
                        for p0 in TAIL_COPIES if rows == TAIL else (0,):
                            sp.dma_start(arow[p0:p0 + rows, s, c0:c1], adj[bass.ds(row0, rows), c0:c1])\
                                .then_inc(me.a_in[s][h], 16)

                def store(t):
                    rows = TAIL if isinstance(t, int) and t == TILES - 1 else P
                    row0 = first_row(t)
                    sp.wait_ge(L[3].row_done, t + 1)
                    if isinstance(t, int):
                        sp.dma_start(out[t * P:t * P + rows, :], xrow[0:rows, t, :]).then_inc(out_stored, 16)
                    else:
                        sp.dma_start(out[bass.ds(row0, P), :],
                                     xrow[:, bass.ds(t, 1), :].rearrange("p a n -> p (a n)"))\
                            .then_inc(out_stored, 16)

                def keep_turned(t, s):
                    for g in range(CHUNKS):
                        r = (2 * s + g) % RING
                        w = P * len(blocks(g))
                        sp.wait_ge(L[0].group_lo, t * CHUNKS + g + 1)
                        sp.dma_start(turned_dram[bass.ds(t, 1), :, :, 512 * g:512 * g + w]
                                     .rearrange("a p h n -> (a p) h n"), pT[:, r, :, 0:w]).then_inc(group_kept[r], 16)

                def keep_and_load(t, s):
                    keep_turned(t - 2, s)
                    load(t, s)

                def load_turned(t, s):
                    if isinstance(t, int) and t < 2:
                        sp.wait_ge(L[2].group_turned, CHUNKS * (TILES - 1 + t))
                    else:
                        sp.wait_ge(L[3].group_used, (t - 1) * CHUNKS)
                    sp.dma_start(turned[:, s, :, :], turned_dram[bass.ds(t, 1), :, :, :]
                                 .rearrange("a p h n -> (a p) h n")).then_inc(L[3].a_in[s][0], 16)

                if l < 3:
                    load(0, 0)
                    load(1, 1)
                    sp.wait_ge(L[l].v_ready, TILES)
                    sp.dma_start(w16[:, :, :, :].rearrange("p h k n -> p (h k n)"), split_dram[V0 + l + 1])\
                        .then_inc(w16_in[l + 1], 16)
                    if l == 0:
                        over_tiles(sp, keep_and_load, first=FIRST)
                        for t in range(LAST, TILES):
                            keep_turned(t, t % 2)
                        for r in range(RING):
                            sp.wait_ge(group_kept[r], 16 * CHUNKS * TILES // RING)
                    else:
                        over_tiles(sp, load, first=FIRST)
                    if is_attention[l + 1]:
                        for i, part in enumerate(parts_in_m16[l + 1]):
                            if l == 0:
                                sp.wait_ge(L[0].counted, TILES)
                            else:
                                sp.wait_ge(L[1].q1_ready, TILES)
                            sp.dma_start(m16[:, i, :, :, :].rearrange("p h k n -> p (h k n)"), split_dram[part])\
                                .then_inc(m16_in[l + 1], 16)
                else:
                    for t in range(4):
                        load_turned(t, t % 2)
                    with sp.Fori(4, LAST - 1, 2) as t:
                        for j in range(2):
                            load_turned(t + j, j)
                            store(t + (j - 4))
                    for t in range(LAST, TILES):
                        load_turned(t, t % 2)
                    for t in range(LAST - 4, TILES):
                        store(t)
            sp.wait_ge(out_stored, 16 * TILES)

        @block.gpsimd
        def _(pool):
            nc.gpsimd.memset(ident[:, :], 0.0).then_inc(ident_zero, 1)
            pool.wait_ge(ident_zero, 1)
            nc.gpsimd.affine_select(out=ident[:, :], in_=ident[:, :], compare_op=ALU.not_equal, fill=1.0,
                                    base=0, pattern=[[-1, P]], channel_multiplier=1).then_inc(ident_set, 1)
            nc.gpsimd.memset(mhalf[:, :], -0.5).then_inc(constants_set, 1)
            nc.gpsimd.memset(ones[:, :], 1.0).then_inc(constants_set, 1)
            pool.wait_ge(bounds_set, 1)
            nc.gpsimd.partition_all_reduce(bound[:, :], amax[:, :], P, RMAX).then_inc(bounds_all, 1)
            for n, which in enumerate(SPLIT_ORDER[:-1]):
                pool.wait_ge(split_lo, n + 1)
                pool.dma_start(split_dram[which].rearrange("p (h n) -> p h n", h=2), split_at[n % 2])\
                    .then_inc(split_stored[n % 2], 16)
                if n == X_PARTS:
                    pool.wait_ge(bounds_set, 2)
                    nc.gpsimd.partition_all_reduce(bound0[:, 2:3], amax0[:, 2:3], P, RMAX).then_inc(bounds_all, 1)

            def stage(l, t, s):
                if l:
                    pool.wait_ge(L[l - 1].row_done, t + 1)
                    if isinstance(t, int) and t < PRESTAGED and is_attention[l - 1]:
                        pool.wait_ge(L[l - 1].scores_ready, CHUNKS * TILES)
                at_least(pool, L[l].x_turned, t - 1)
                nc.gpsimd.tensor_copy(x_stage[s], xrow[:, bass.ds(t, 1), :].rearrange("p a n -> p (a n)"))\
                    .then_inc(L[l].x_staged, 1)

            def rstd_of(l, t):
                pool.wait_ge(L[l].var_ready, t + 1)
                nc.gpsimd.tensor_tensor(rstd[:, :], vareps[:, :], mhalf[:, 0:1], ALU.pow).then_inc(L[l].rstd_ready, 1)

            pool.wait_ge(x_in, X_LOADS * 16)
            for t in range(PRESTAGED):
                stage(0, t, t % 2)
            for l in LAYERS:
                with pool.Fori(PRESTAGED, LAST - 1, 2) as t:
                    stage(l, t, 0)
                    stage(l, t + 1, 1)
                for t in range(LAST, TILES):
                    stage(l, t, t % 2)
                if l == 0:
                    pool.wait_ge(constants_set, 1)
                    pool.wait_ge(pow_wanted, 1)
                    nc.gpsimd.tensor_tensor(dis[:, :], tmp[:, :], mhalf[:, :], ALU.pow).then_inc(pow_done, 1)
                    pool.wait_ge(bounds_set, 3)
                    nc.gpsimd.partition_all_reduce(bound0[:, 0:2], amax0[:, 0:2], P, RMAX).then_inc(bounds_all, 1)
                with pool.Fori(0, TILES - 1) as t:
                    rstd_of(l, t)
                if l < 3:
                    for t in range(PRESTAGED):
                        stage(l + 1, t, t % 2)
                rstd_of(l, TILES - 1)

        @block.tensor
        def _(pe):
            job = [0]

            def begin_job():
                at_least(pe, job_taken, job[0] - 7)
                b = bank[job[0] % 8]
                job[0] += 1
                return b

            def turn_weights(i):
                pe.wait_ge(w_in[i], 16)
                for o in range(KD):
                    b = begin_job()
                    for k in range(KD):
                        last = nc.tensor.transpose(b[:, k * P:(k + 1) * P], slot3(i)[:, k, o * P:(o + 1) * P], ident[:, :])
                    last.then_inc(job_done, 1)

            def product(left, right):
                for i in range(KD):
                    b = begin_job()
                    for k in range(KD):
                        last = nc.tensor.matmul(b[:, :], slot3(left)[:, k, i * P:(i + 1) * P], slot3(right)[:, k, :],
                                                start=(k == 0), stop=(k == KD - 1))
                    last.then_inc(job_done, 1)

            pe.wait_ge(ident_set, 1)
            turn_weights(WK1)
            pe.wait_ge(w_in[WQ2], 16)
            pe.wait_ge(w_in[WK2], 16)
            product(WQ2, WK2)
            pe.wait_ge(small_in, 16 * 5)
            pe.wait_ge(dve_step, 1)
            b = begin_job()
            for k in range(KD):
                last = nc.tensor.matmul(b[:, :], bk_wide[:, k, :], slot3(WQ2)[:, k, :], start=(k == 0), stop=(k == KD - 1))
            last.then_inc(job_done, 1)
            b = begin_job()
            for j in range(KD + 1):
                for k in range(KD):
                    left = slot3(WK2)[:, k, j * P:(j + 1) * P] if j < KD else bk_wide[:, k, :]
                    last = nc.tensor.matmul(b[:, j:j + 1], left, bcol[:, 0, k:k + 1], start=(k == 0), stop=(k == KD - 1))
            last.then_inc(job_done, 1)
            turn_weights(WV2)
            turn_weights(W0)

            for l in LAYERS:
                me = L[l]

                def turn_x(t, s, l=l):
                    me = L[l]
                    if l and isinstance(t, int) and t < 2:
                        pe.wait_ge(L[l - 1].group_lo, CHUNKS * TILES - 1 + t)
                    at_least(pe, me.xT_lo, t - 1)
                    pe.wait_ge(me.x_staged, t + 1)
                    for k in range(KD):
                        last = nc.tensor.transpose(turn_bank[s][:, k * P:(k + 1) * P],
                                                   x_stage[s][:, k * P:(k + 1) * P], ident[:, :])
                    last.then_inc(me.x_turned, 1)

                def project(t, s):
                    if not (isinstance(t, int) and (t == TILES - 1 or l and t == 0)):
                        turn_x(t + 1, 1 - s)
                    pe.wait_ge(me.xT_lo, t + 1)
                    at_least(pe, me.v_lo if l else me.v_kept, t - 1)
                    if l and isinstance(t, int) and t < 2:
                        pe.wait_ge(L[l - 1].out_taken, TILES - 1 + t)
                    n = 0
                    for xh, wh in ((0, 0), (0, 1), (1, 0)):
                        for k in range(KD):
                            last = nc.tensor.matmul(out_bank[s][:, :], xT[:, xh, k, bass.ds(t * P, P)],
                                                    w16[:, wh, k, :], start=(n == 0), stop=(n == 3 * KD - 1))
                            n += 1
                    last.then_inc(me.v_ready, 1)

                def turn_group(t, s, g):
                    G = t * CHUNKS + g
                    at_least(pe, me.group_lo, G - 1)
                    if is_attention[l]:
                        if g == 0:
                            pe.wait_ge(me.probs_ready, t + 1)
                    elif g in (0, HALF):
                        pe.wait_ge(me.a_in[s][g // HALF], loaded(t, s))
                    if g == CHUNKS - 1 and not is_attention[l]:
                        pe.wait_ge(me.tail_copied, t + 1)
                    b = turn_bank[g % 2]
                    for n, k in enumerate(blocks(g)):
                        last = nc.tensor.transpose(b[:, n * P:(n + 1) * P], arow[:, s, k * P:(k + 1) * P], ident[:, :])
                    last.then_inc(me.group_turned, 1)

                def use_group(t, s, g):
                    G = t * CHUNKS + g
                    r = (2 * s + g) % RING
                    if g == 0:
                        at_least(pe, me.out_taken, t - 1)
                        if isinstance(t, int) and t == 0 and l:
                            pe.wait_ge(me.v_lo, TILES - 1)
                    if isinstance(t, int) and t == 0:
                        pe.wait_ge(me.v_lo, blocks(g)[-1] + 1)
                    if l < 3:
                        pe.wait_ge(me.group_lo, G + 1)
                    elif g == 0:
                        pe.wait_ge(me.a_in[s][0], (t - s) * 8 + 16)
                    for n, k in enumerate(blocks(g)):
                        for ph, vh in ((0, 0), (0, 1), (1, 0)) if k < TILES - 1 else ((0, 0),):
                            left = pT[:, r, ph, n * P:(n + 1) * P] if l < 3 else turned[:, s, ph, k * P:(k + 1) * P]
                            last = nc.tensor.matmul(out_bank[s][:, :], left, v16[:, k, vh, :],
                                                    start=(k == 0 and ph + vh == 0), stop=(k == TILES - 1))
                    last.then_inc(me.group_used, 1)

                def weigh(part, right):
                    for j in range(KD):
                        n = 0
                        for mh, xh in ((0, 0), (0, 1), (1, 0)):
                            for k in range(KD):
                                last = nc.tensor.matmul(q_bank[:, j * P:(j + 1) * P], m16[:, part, mh, k, j * P:(j + 1) * P],
                                                        right(xh, k), start=(n == 0), stop=(n == 3 * KD - 1))
                                n += 1
                    return last

                def first_query(t):
                    at_least(pe, me.q_lo, t)
                    weigh(0, lambda xh, k: xT[:, xh, k, bass.ds(t * P, P)]).then_inc(me.q1_ready, 1)

                def query(t, s):
                    if l == 1:
                        pe.wait_ge(me.q1_lo, t + 1)
                        weigh(1, lambda xh, k: q1T[:, xh, k, :]).then_inc(me.q_ready, 1)
                    else:
                        at_least(pe, me.q_lo, t)
                        weigh(0, lambda xh, k: xT[:, xh, k, bass.ds(t * P, P)]).then_inc(me.q_ready, 1)

                def scores(t, s, c):
                    if c == 0:
                        pe.wait_ge(me.q_lo, t + 1)
                    at_least(pe, me.scores_taken, t * CHUNKS + c - 2)
                    n, w = 0, width(c)
                    for qh, xh in ((0, 0), (0, 1), (1, 0)):
                        for k in range(KD):
                            last = nc.tensor.matmul(score_bank[c % 3][:, 0:w], qT[:, s, qh, k, :],
                                                    xT[:, xh, k, 512 * c:512 * c + w], start=(n == 0), stop=(n == 3 * KD - 1))
                            n += 1
                    last.then_inc(me.scores_ready, 1)

                def rows(t, s):
                    last_tile = isinstance(t, int) and t == TILES - 1
                    if is_attention[l]:
                        for c in range(CHUNKS):
                            if c >= CHUNKS - 2 and not last_tile:
                                turn_group(t, s, c - (CHUNKS - 2))
                            if not last_tile:
                                scores(t + 1, 1 - s, c)
                                if not (isinstance(t, int) and t >= LAST):
                                    if c == 0 and l == 1:
                                        first_query(t + 2)
                                    if c == 2:
                                        query(t + 2, s)
                    for g in range(CHUNKS):
                        if l == 3:
                            pass
                        elif g + 2 < CHUNKS:
                            turn_group(t, s, g + 2)
                        elif isinstance(t, int) and t == TILES - 2 or not is_attention[l] and not last_tile:
                            turn_group(t + 1, 1 - s, g + 2 - CHUNKS)
                        if last_tile and l < 3 and g >= CHUNKS - 2:
                            turn_x(g - (CHUNKS - 2), g % 2, l + 1)
                        use_group(t, s, g)

                if l:
                    pe.wait_ge(w16_in[l], 16)
                else:
                    pe.wait_ge(split_lo, len(SPLIT_ORDER))
                    turn_x(0, 0)
                over_tiles(pe, project, end=TILES - 1)
                if is_attention[l]:
                    pe.wait_ge(m16_in[l], 16 * len(parts_in_m16[l]))
                    first_query(0) if l == 1 else query(0, 0)
                    project(TILES - 1, 1)
                    if l == 1:
                        query(0, 0)
                    for c in range(CHUNKS):
                        scores(0, 0, c)
                        if c == 0 and l == 1:
                            first_query(1)
                        if c == 2:
                            query(1, 1)
                else:
                    project(TILES - 1, 1)
                    if l == 0:
                        turn_group(0, 0, 0)
                        turn_group(0, 0, 1)
                over_tiles(pe, rows)

        @block.scalar
        def _(act):
            job = [0]

            def take_job(dst, factor=1.0):
                act.wait_ge(job_done, job[0] + 1)
                b = bank[job[0] % 8]
                job[0] += 1
                nc.scalar.activation(dst, b[:, 0:dst.shape[-1]], ACT.Copy, scale=factor).then_inc(job_taken, 1)

            for o in range(KD):
                take_job(slot3(WK1T)[:, o, :])
            for o in range(KD):
                take_job(slot3(M2_SLOT)[:, o, :], RSQRT_D)
            take_job(ubk[:, :], RSQRT_D)
            take_job(vq[:, :], RSQRT_D)
            def sum_abs(t, s):
                act.wait_ge(a0_in[s], loaded(t, s))
                at_least(act, summed_abs, t)
                nc.scalar.activation(junk, arow[:, s, 0:N], ACT.Abs,
                                     accum_out=rabs[:, t:t + 1] if isinstance(t, int) else rabs[:, bass.ds(t, 1)])\
                    .then_inc(summed_abs, 1)

            sum_abs(0, 0)
            for i in (WV2T, W0T):
                for o in range(KD):
                    take_job(slot3(i)[:, o, :])
            sum_abs(1, 1)
            act.wait_ge(scales_set, 1)
            for n, which in enumerate(SPLIT_ORDER):
                if n >= 2:
                    act.wait_ge(split_stored[n % 2], 16 * (n // 2))
                if which in (V1, V3, Q1):
                    act.wait_ge(w_in[final[which]], 16)
                nc.scalar.activation(split_at[n % 2][:, 0, :], slot(final[which]), ACT.Copy,
                                     scale=scale[:, which:which + 1]).then_inc(split_hi, 1)
                if n in SUM_AFTER_SPLIT:
                    t = 2 + SUM_AFTER_SPLIT.index(n)
                    sum_abs(t, t % 2)

            for l in LAYERS:
                me = L[l]
                x_factor = scale0[:, 2:3] if l == 0 else 2.0 ** X_BITS

                def turned_hi(t, s):
                    if l == 0 and t == 0:
                        act.wait_ge(x_scale_set, 1)
                    act.wait_ge(me.x_turned, t + 1)
                    nc.scalar.activation(xT[:, 0, :, bass.ds(t * P, P)], cols3(turn_bank[s][:, :]), ACT.Copy,
                                         scale=x_factor).then_inc(me.xT_hi, 1)

                def project(t, s, sum_tile=None):
                    if not (isinstance(t, int) and t == TILES - 1):
                        turned_hi(t + 1, 1 - s)
                    if sum_tile is not None:
                        sum_abs(sum_tile, sum_tile % 2)
                    act.wait_ge(me.v_ready, t + 1)
                    if l == 0:
                        nc.scalar.activation(v_whole(t), out_bank[s][:, :], ACT.Copy).then_inc(me.v_kept, 1)
                    else:
                        nc.scalar.activation(v16[:, bass.ds(t, 1), 0, :].rearrange("p a n -> p (a n)"), out_bank[s][:, :],
                                             ACT.Copy, scale=V_SHIFT).then_inc(me.v_hi, 1)

                def kept_v_hi(k):
                    at_least(act, me.v_lo, k - 1)
                    nc.scalar.activation(v16[:, k, 0, :], v_whole(k), ACT.Copy, scale=kz[:, k:k + 1]).then_inc(me.v_hi, 1)

                def group_hi(t, s, g):
                    G = t * CHUNKS + g
                    r = (2 * s + g) % RING
                    act.wait_ge(me.group_turned, G + 1)
                    at_least(act, me.group_used, G - RING + 1)
                    if l == 0:
                        at_least(act, group_kept[r], (t - s) * (8 * CHUNKS // RING * 2) + 16 * ((s * CHUNKS + g) // RING))
                    w = P * len(blocks(g))
                    nc.scalar.activation(pT[:, r, 0, 0:w], turn_bank[g % 2][:, 0:w], ACT.Copy,
                                         scale=2.0 ** P_BITS if is_attention[l] else scale0[:, 1:2])\
                        .then_inc(me.group_hi, 1)

                def query_hi(t, s):
                    act.wait_ge(me.q_ready, t + 1)
                    at_least(act, me.scores_ready, (t - 1) * CHUNKS)
                    for j in range(KD):
                        if l == 2:
                            last = nc.scalar.activation(qT[:, s, 0, j, :], q_bank[:, j * P:(j + 1) * P], ACT.Identity,
                                                        scale=V_SHIFT, bias=vq[:, j:j + 1])
                        elif j == 0:
                            last = nc.scalar.activation(qT[:, s, 0, :, :], cols3(q_bank[:, :]), ACT.Copy, scale=Q1_SHIFT)
                    last.then_inc(me.q_hi, 1)

                def first_query_hi(t):
                    act.wait_ge(me.q1_ready, t + 1)
                    at_least(act, me.q_ready, t)
                    nc.scalar.activation(q1T[:, 0, :, :], cols3(q_bank[:, :]), ACT.Copy, scale=V_SHIFT)\
                        .then_inc(me.q1_hi, 1)

                def exps(t, s):
                    act.wait_ge(me.rowmax_ready, t + 1)
                    at_least(act, me.out_taken, t - 1)
                    nc.scalar.activation(arow[:, s, 0:N], arow[:, s, 0:N], ACT.Exp, bias=negmax[:, s:s + 1],
                                         scale=const[:, 0:1], accum_out=rowsum[:, s:s + 1]).then_inc(me.exps_done, 1)
                    act.wait_ge(me.exps_done, t + 1)
                    copy_tail_columns(s).then_inc(me.probs_ready, 1)

                def rows(t, s):
                    last_tile = isinstance(t, int) and t == TILES - 1
                    before_last = isinstance(t, int) and t == TILES - 2
                    if is_attention[l] and not (isinstance(t, int) and t >= LAST):
                        if l == 1:
                            first_query_hi(t + 2)
                        query_hi(t + 2, s)
                    for g in range(CHUNKS):
                        if g == 2 and not is_attention[l]:
                            act.wait_ge(me.a_in[s][1], loaded(t, s))
                            copy_tail_columns(s).then_inc(me.tail_copied, 1)
                        group_hi(t, s, g)
                        if l == 0 and isinstance(t, int) and t == 0:
                            for k in blocks(g):
                                kept_v_hi(k)
                        if g == CHUNKS - 3 and before_last or g == CHUNKS - 1 and not before_last and not last_tile:
                            if is_attention[l]:
                                exps(t + 1, 1 - s)

                turned_hi(0, 0)
                if l == 0:
                    for t in range(TILES_SPLIT, TILES):
                        first = projected_by(t - 1)
                        for done in range(first, projected_by(t)):
                            project(done, done % 2, t if done == first else None)
                    project(TILES - 2, 0)
                else:
                    over_tiles(act, project, end=TILES - 1)
                if is_attention[l]:
                    first_query_hi(0) if l == 1 else query_hi(0, 0)
                    project(TILES - 1, 1)
                    if l == 1:
                        query_hi(0, 0)
                        first_query_hi(1)
                    query_hi(1, 1)
                    exps(0, 0)
                else:
                    project(TILES - 1, 1)
                if l == 0:
                    act.wait_ge(factors_set, 1)
                    for i in range(2):
                        act.wait_ge(split_stored[i], 16 * 3)
                    act.wait_ge(me.v_kept, TILES)
                if l < 3:
                    over_tiles(act, rows)

        @block.vector
        def _(dve):
            steps = [0]

            def step(ins):
                ins.then_inc(dve_step, 1)
                steps[0] += 1
                dve.wait_ge(dve_step, steps[0])

            def powers(bound_, scale_, inv_, tops):
                w = len(tops)
                step(nc.vector.tensor_scalar(inv_[:, 0:w], bound_[:, 0:w], 2.0 ** -100, 2.0 ** 100, ALU.max, ALU.min))
                step(nc.vector.tensor_scalar(inv_[:, 0:w].bitcast(I32), inv_[:, 0:w].bitcast(I32), EXP_MASK, None,
                                             ALU.bitwise_and))
                step(nc.vector.reciprocal(scale_[:, 0:w], inv_[:, 0:w]))
                first = 0
                for i, top in enumerate(tops):
                    if i + 1 == w or tops[i + 1] != top:
                        run = slice(first, i + 1)
                        first = i + 1
                        if top:
                            step(nc.vector.tensor_scalar(scale_[:, run], scale_[:, run], 2.0 ** top, None, ALU.mult))
                            step(nc.vector.tensor_scalar(inv_[:, run], inv_[:, run], 2.0 ** -top, None, ALU.mult))

            dve.wait_ge(small_in, 16 * 5)
            dve.wait_ge(constants_set, 2)
            for k in range(KD):
                last = nc.vector.tensor_scalar(bk_wide[:, k, :], ones[:, :], bcol[:, 1, k:k + 1], None, ALU.mult)
            step(last)
            nc.vector.memset(xrow[:, TILES - 1, :], 0.0).then_inc(pads_zero, 1)
            for s in range(2):
                nc.vector.memset(arow[:, s, N:NP], 0.0).then_inc(pads_zero, 1)

            def sum_row(t, s):
                dve.wait_ge(a0_in[s], loaded(t, s))
                nc.vector.tensor_reduce(deg[:, t:t + 1] if isinstance(t, int) else deg[:, bass.ds(t, 1)],
                                        arow[:, s, 0:N], AX.X, ALU.add).then_inc(summed, 1)

            def largest(i, numbers):
                return nc.vector.tensor_reduce(amax[:, i:i + 1], numbers, AX.X, ALU.max, apply_absolute_value=True)

            dve.wait_ge(job_taken, 4)
            largest(K1, slot(WK1T))
            for i, w in ((V2, WV2), (V0, W0), (Q1, WQ1), (V1, WV1), (V3, W3)):
                dve.wait_ge(w_in[w], 16)
                largest(i, slot(w))
            for t in range(2):
                sum_row(t, t)
            dve.wait_ge(job_taken, 10)
            largest(M2, slot(M2_SLOT))
            step(largest(7, vq[:, 0:KD]))
            nc.vector.tensor_scalar(amax[:, 7:8], amax[:, 7:8], 2.0 ** -9, None, ALU.mult).then_inc(bounds_set, 1)
            dve.wait_ge(bounds_all, 1)
            step(nc.vector.tensor_tensor(bound[:, M2:M2 + 1], bound[:, M2:M2 + 1], bound[:, 7:8], ALU.max))
            powers(bound, scale, inv, [W_TOP] * 6 + [M_TOP])
            nc.vector.tensor_scalar(vq[:, 0:KD], vq[:, 0:KD], scale[:, M2:M2 + 1], 2.0 ** -9, ALU.mult, ALU.mult)\
                .then_inc(scales_set, 1)
            dve.wait_ge(job_taken, 18)
            for n, which in enumerate(SPLIT_ORDER):
                if n == len(SPLIT_ORDER) - 1:
                    dve.wait_ge(bounds_all, 2)
                    powers(bound0[:, 2:3], scale0[:, 2:3], inv0[:, 2:3], [W_TOP])
                    dve.drain().then_inc(x_scale_set, 1)
                dve.wait_ge(split_hi, n + 1)
                nc.vector.scalar_tensor_tensor(split_at[n % 2][:, 1, :], slot(final[which]), scale[:, which:which + 1],
                                               split_at[n % 2][:, 0, :], ALU.mult, ALU.subtract).then_inc(split_lo, 1)
                if n in SUM_AFTER_SPLIT:
                    t = 2 + SUM_AFTER_SPLIT.index(n)
                    sum_row(t, t % 2)
                if n == 0:
                    dve.wait_ge(x_in, X_LOADS * 16)
                if n < X_PARTS:
                    part = xrow[:, x_part[n][0]:x_part[n][-1] + 1, :].rearrange("p t n -> p (t n)")
                    nc.vector.tensor_reduce(xmax[:, n:n + 1], part, AX.X, ALU.max, apply_absolute_value=True)\
                        .then_inc(dve_step, 1)
                    steps[0] += 1
                elif n == X_PARTS:
                    dve.wait_ge(dve_step, steps[0])
                    nc.vector.tensor_reduce(amax0[:, 2:3], xmax[:, :], AX.X, ALU.max).then_inc(bounds_set, 1)

            def degree_factors():
                dve.wait_ge(summed_abs, TILES)
                step(nc.vector.tensor_reduce(amax0[:, 1:2], rabs[:, :], AX.X, ALU.max))
                dve.wait_ge(pow_done, 1)
                nc.vector.tensor_reduce(amax0[:, 0:1], dis[:, :], AX.X, ALU.max).then_inc(bounds_set, 1)
                dve.wait_ge(bounds_all, 3)
                powers(bound0, scale0, inv0, [0, W_TOP])
                nc.vector.tensor_scalar(kz[:, :], dis[:, :], scale0[:, 0:1], 2.0 ** -25, ALU.mult, ALU.mult)\
                    .then_inc(factors_set, 1)
                dve.wait_ge(factors_set, 1)
                step(nc.vector.tensor_scalar(kout[:, :], dis[:, :], inv0[:, 0:1], inv0[:, 1:2], ALU.mult, ALU.mult))
                step(nc.vector.tensor_scalar(kout[:, :], kout[:, :], inv0[:, 2:3], inv[:, V0:V0 + 1], ALU.mult, ALU.mult))
                step(nc.vector.tensor_scalar(kout[:, :], kout[:, :], 2.0 ** 25, None, ALU.mult))

            for l in LAYERS:
                me = L[l]

                def row(buf, t):
                    return buf[:, t, :] if isinstance(t, int) else buf[:, bass.ds(t, 1), :].rearrange("p a n -> p (a n)")

                def set_constants():
                    if is_attention[l]:
                        if l == 1:
                            step(nc.vector.tensor_scalar(const[:, 0:1], inv[:, Q1:Q1 + 1], inv[:, K1:K1 + 1], None, ALU.mult))
                            step(nc.vector.tensor_scalar(const[:, 0:1], const[:, 0:1], RSQRT_D * 2.0 ** 23, None, ALU.mult))
                        else:
                            step(nc.vector.tensor_scalar(const[:, 0:1], inv[:, M2:M2 + 1], 0.5, None, ALU.mult))
                            step(nc.vector.tensor_scalar(const[:, 1:2], scale[:, M2:M2 + 1], 4.0, None, ALU.mult))
                        step(nc.vector.tensor_scalar(const[:, 2:3], inv[:, V0 + l:V0 + l + 1], 2.0 ** (9 - P_BITS), None, ALU.mult))
                    if l == 3:
                        step(nc.vector.tensor_scalar(tmp[:, :], count[:, :], 1.0, None, ALU.max))
                        step(nc.vector.reciprocal(invdeg[:, :], tmp[:, :]))
                        step(nc.vector.tensor_scalar(const[:, 0:1], inv[:, V3:V3 + 1], 2.0 ** 9, None, ALU.mult))
                        step(nc.vector.tensor_scalar(kout[:, :], invdeg[:, :], inv0[:, 1:2], const[:, 0:1], ALU.mult, ALU.mult))
                        step(nc.vector.tensor_scalar(kself[:, :], invdeg[:, :], 1.0, const[:, 0:1], ALU.add, ALU.mult))

                def turned_lo(t, s, l=l):
                    me = L[l]
                    x_factor = scale0[:, 2:3] if l == 0 else 2.0 ** X_BITS
                    dve.wait_ge(me.xT_hi, t + 1)
                    nc.vector.scalar_tensor_tensor(xT[:, 1, :, bass.ds(t * P, P)], cols3(turn_bank[s][:, :]), x_factor,
                                                   xT[:, 0, :, bass.ds(t * P, P)], ALU.mult, ALU.subtract)\
                        .then_inc(me.xT_lo, 1)

                def project(t, s):
                    if not (isinstance(t, int) and (t == TILES - 1 or l and t == 0)):
                        turned_lo(t + 1, 1 - s)
                    if l:
                        v_lo(t, out_bank[s], V_SHIFT)

                def v_lo(t, whole_v, factor):
                    dve.wait_ge(me.v_hi, t + 1)
                    lo = nc.vector.scalar_tensor_tensor(row(v16[:, :, 1, :], t), whole_v[:, :], factor,
                                                        row(v16[:, :, 0, :], t), ALU.mult, ALU.subtract)
                    if isinstance(t, int) and t == TILES - 1:
                        lo.then_inc(tail_split, 1)
                        dve.wait_ge(tail_split, l + 1)
                        second = v16[32:64, t, 0, :]
                        lo = nc.vector.scalar_tensor_tensor(second, whole_v[32:64, :], factor if l else factor[32:64],
                                                            second, ALU.mult, ALU.subtract)
                    lo.then_inc(me.v_lo, 1)

                def group_lo(t, s, g):
                    G = t * CHUNKS + g
                    r = (2 * s + g) % RING
                    dve.wait_ge(me.group_hi, G + 1)
                    w = P * len(blocks(g))
                    factor = 2.0 ** P_BITS if is_attention[l] else scale0[:, 1:2]
                    lo = nc.vector.scalar_tensor_tensor(pT[:, r, 1, 0:w], turn_bank[g % 2][:, 0:w], factor,
                                                        pT[:, r, 0, 0:w], ALU.mult, ALU.subtract)
                    if g == CHUNKS - 1:
                        lo.then_inc(me.last_lo, 1)
                        dve.wait_ge(me.last_lo, t + 1)
                        third = pT[64:96, r, 0, w - P:w]
                        lo = nc.vector.scalar_tensor_tensor(third, turn_bank[g % 2][64:96, w - P:w],
                                                            factor if is_attention[l] else factor[64:96], third,
                                                            ALU.mult, ALU.subtract)
                    lo.then_inc(me.group_lo, 1)

                def query_lo(t, s):
                    dve.wait_ge(me.q_hi, t + 1)
                    if l == 2:
                        for j in range(KD):
                            last = nc.vector.tensor_scalar(upd[:, j * P:(j + 1) * P], q_bank[:, j * P:(j + 1) * P], V_SHIFT,
                                                           vq[:, j:j + 1], ALU.mult, ALU.add)
                        last.then_inc(me.q_step, 1)
                        dve.wait_ge(me.q_step, t + 1)
                        nc.vector.tensor_tensor(qT[:, s, 1, :, :], cols3(upd[:, :]), qT[:, s, 0, :, :],
                                                ALU.subtract).then_inc(me.q_lo, 1)
                    else:
                        nc.vector.scalar_tensor_tensor(qT[:, s, 1, :, :], cols3(q_bank[:, :]), Q1_SHIFT, qT[:, s, 0, :, :],
                                                       ALU.mult, ALU.subtract).then_inc(me.q_lo, 1)

                def first_query_lo(t):
                    dve.wait_ge(me.q1_hi, t + 1)
                    nc.vector.scalar_tensor_tensor(q1T[:, 1, :, :], cols3(q_bank[:, :]), V_SHIFT, q1T[:, 0, :, :],
                                                   ALU.mult, ALU.subtract).then_inc(me.q1_lo, 1)

                TILE_STEPS = CHUNKS + (4 if l == 2 else 1)

                def scores_taken(t, s, c):
                    if c in (0, HALF):
                        dve.wait_ge(me.a_in[s][c // HALF], loaded(t, s))
                    dve.wait_ge(me.scores_ready, t * CHUNKS + c + 1)
                    a = arow[:, s, 512 * c:512 * c + width(c)]
                    b = score_bank[c % 3][:, 0:width(c)]
                    if l == 1:
                        nc.vector.tensor_tensor(a, b, a, ALU.mult).then_inc(me.scores_taken, 1)
                    else:
                        nc.vector.scalar_tensor_tensor(a, a, const[:, 1:2], b, ALU.mult, ALU.add)\
                            .then_inc(me.scores_taken, 1)

                def chunk_max(t, s, c):
                    dve.wait_ge(me.scores_taken, t * CHUNKS + c + 1)
                    nc.vector.tensor_reduce(cmax[:, s, c:c + 1], arow[:, s, 512 * c:512 * c + width(c)], AX.X, ALU.max)\
                        .then_inc(me.max_step, 1)

                def row_max(t, s):
                    n = t * TILE_STEPS + CHUNKS
                    dve.wait_ge(me.max_step, n)
                    top = tiny[:, 1:2]
                    nc.vector.tensor_reduce(top, cmax[:, s, :], AX.X, ALU.max).then_inc(me.max_step, 1)
                    dve.wait_ge(me.max_step, n + 1)
                    if l == 1:
                        nc.vector.tensor_scalar(negmax[:, s:s + 1], top, const[:, 0:1], -1.0, ALU.mult, ALU.mult)\
                            .then_inc(me.rowmax_ready, 1)
                        return
                    r, r_all, logit_max = tiny[:, 2:3], tiny[:, 3:4], tiny[:, 4:5]
                    nc.vector.scalar_tensor_tensor(junk[:, 0:D], row(xrow, t), 1.0, ubk[:, :], ALU.mult, ALU.mult,
                                                   accum_out=r).then_inc(me.max_step, 1)
                    dve.wait_ge(me.max_step, n + 2)
                    nc.vector.tensor_tensor(r_all, r, vq[:, KD:KD + 1], ALU.add).then_inc(me.max_step, 1)
                    dve.wait_ge(me.max_step, n + 3)
                    nc.vector.tensor_scalar(logit_max, top, const[:, 0:1], r_all, ALU.mult, ALU.add)\
                        .then_inc(me.max_step, 1)
                    dve.wait_ge(me.max_step, n + 4)
                    nc.vector.tensor_tensor(negmax[:, s:s + 1], r_all, logit_max, ALU.subtract)\
                        .then_inc(me.rowmax_ready, 1)

                NORM_STEPS = (2, 3, 4, 4)[l]

                def update(t, s):
                    n = [t * NORM_STEPS]

                    def norm_step(ins):
                        ins.then_inc(me.norm_step, 1)
                        n[0] = n[0] + 1
                        dve.wait_ge(me.norm_step, n[0])

                    acc = out_bank[s][:, :]
                    dve.wait_ge(me.group_used, (t + 1) * CHUNKS)
                    if is_attention[l]:
                        dve.wait_ge(me.probs_ready, t + 1)
                        norm_step(nc.vector.reciprocal(tiny[:, 5:6], rowsum[:, s:s + 1]))
                        norm_step(nc.vector.tensor_tensor(tiny[:, 6:7], tiny[:, 5:6], const[:, 2:3], ALU.mult))
                        nc.vector.scalar_tensor_tensor(y[:, :], acc, tiny[:, 6:7], row(xrow, t), ALU.mult, ALU.add)\
                            .then_inc(me.out_taken, 1)
                        dve.wait_ge(me.out_taken, t + 1)
                        if l == 2:
                            norm_step(nc.vector.tensor_tensor(y[:, :], y[:, :], bias[:, 1, :], ALU.add))
                    elif l == 0:
                        nc.vector.scalar_tensor_tensor(y[:, :], acc, kout[:, bass.ds(t, 1)], row(xrow, t), ALU.mult, ALU.add)\
                            .then_inc(me.out_taken, 1)
                        dve.wait_ge(me.out_taken, t + 1)
                        norm_step(nc.vector.tensor_tensor(y[:, :], y[:, :], bias[:, 0, :], ALU.add))
                    else:
                        norm_step(nc.vector.tensor_tensor(upd[:, :], row(v16[:, :, 0, :], t), row(v16[:, :, 1, :], t), ALU.add))
                        norm_step(nc.vector.scalar_tensor_tensor(upd[:, :], upd[:, :], kself[:, bass.ds(t, 1)], bias[:, 2, :],
                                                                 ALU.mult, ALU.add))
                        nc.vector.scalar_tensor_tensor(upd[:, :], acc, kout[:, bass.ds(t, 1)], upd[:, :], ALU.mult, ALU.add)\
                            .then_inc(me.out_taken, 1)
                        dve.wait_ge(me.out_taken, t + 1)
                        norm_step(nc.vector.scalar_tensor_tensor(y[:, :], upd[:, :], 0.0, row(xrow, t), ALU.max, ALU.add))
                    nc.vector.bn_stats(st6[:, :], y[:, :])
                    dve.drain()
                    norm_step(nc.vector.bn_aggr(mv[:, :], st6[:, :]))
                    nc.vector.tensor_scalar(vareps[:, :], mv[:, 1:2], LN_EPS, None, ALU.add).then_inc(me.var_ready, 1)

                def normalise(t):
                    dve.wait_ge(me.rstd_ready, t + 1)
                    nc.vector.tensor_scalar(row(xrow, t), y[:, :], mv[:, 0:1], rstd[:, 0:1], ALU.subtract, ALU.mult)\
                        .then_inc(me.row_done, 1)

                def rows(t, s):
                    first = isinstance(t, int) and t == 0
                    last_tile = isinstance(t, int) and t == TILES - 1
                    if is_attention[l] and last_tile:
                        for g in range(CHUNKS):
                            group_lo(t, s, g)
                            if g == 1:
                                update(t - 1, 1 - s)
                            if g == 2:
                                normalise(t - 1)
                        return
                    if is_attention[l]:
                        for c in range(CHUNKS):
                            if c >= CHUNKS - 2:
                                group_lo(t, s, c - (CHUNKS - 2))
                            if not last_tile:
                                scores_taken(t + 1, 1 - s, c)
                                if not (isinstance(t, int) and t >= LAST):
                                    if c == 0 and l == 1:
                                        first_query_lo(t + 2)
                                    if c == 2:
                                        query_lo(t + 2, s)
                                if c:
                                    chunk_max(t + 1, 1 - s, c - 1)
                            if c == 0 and not first:
                                update(t - 1, 1 - s)
                            if c == 3 and not first:
                                normalise(t - 1)
                        if not last_tile:
                            chunk_max(t + 1, 1 - s, CHUNKS - 1)
                        for g in range(2, CHUNKS):
                            group_lo(t, s, g)
                            if g == 2 and not last_tile:
                                row_max(t + 1, 1 - s)
                        return
                    for g in range(CHUNKS):
                        if l < 3:
                            group_lo(t, s, g)
                        if l == 0 and first:
                            for k in blocks(g):
                                v_lo(k, v_whole(k), kz[:, k:k + 1])
                        if g == 1 and not first:
                            update(t - 1, 1 - s)
                        if g == 3 and not first:
                            normalise(t - 1)
                        if l == 0 and g == 4:
                            for h in range(2):
                                dve.wait_ge(me.a_in[s][h], loaded(t, s))
                            nc.vector.tensor_scalar(junk, arow[:, s, 0:N], 0.0, None, ALU.not_equal, ALU.add,
                                                    accum_out=count[:, bass.ds(t, 1)]).then_inc(me.counted, 1)

                set_constants()
                if l == 0:
                    turned_lo(0, 0)
                    for t in range(TILES_SPLIT, TILES):
                        first = projected_by(t - 1)
                        project(first, first % 2)
                        sum_row(t, t % 2)
                        if t == TILES - 1:
                            dve.wait_ge(summed, TILES)
                            nc.vector.tensor_scalar(tmp[:, :], deg[:, :], DEG_EPS, None, ALU.add).then_inc(pow_wanted, 1)
                        for done in range(first + 1, projected_by(t)):
                            project(done, done % 2)
                    project(TILES - 2, 0)
                else:
                    over_tiles(dve, project, end=TILES - 1)
                if is_attention[l]:
                    first_query_lo(0) if l == 1 else query_lo(0, 0)
                    project(TILES - 1, 1)
                    if l == 1:
                        query_lo(0, 0)
                    for c in range(CHUNKS):
                        scores_taken(0, 0, c)
                        if c == 0 and l == 1:
                            first_query_lo(1)
                        if c == 2:
                            query_lo(1, 1)
                        if c:
                            chunk_max(0, 0, c - 1)
                    chunk_max(0, 0, CHUNKS - 1)
                    row_max(0, 0)
                else:
                    project(TILES - 1, 1)
                if l == 0:
                    degree_factors()
                over_tiles(dve, rows)
                if l < 3:
                    turned_lo(0, 0, l + 1)
                    turned_lo(1, 1, l + 1)
                update(TILES - 1, (TILES - 1) % 2)
                normalise(TILES - 1)


_INS = ["x", "adj", "L0_gnn_W", "L0_gnn_b", "L1_gnn_W_Q", "L1_gnn_W_K", "L1_gnn_W_V", "L2_gnn_Wq", "L2_gnn_bq",
        "L2_gnn_Wk", "L2_gnn_bk", "L2_gnn_Wv", "L2_gnn_bv", "L3_gnn_W", "L3_gnn_b"]


def kernel(**inputs):
    import numpy as _np
    import concourse.bacc as _bacc
    from concourse import mybir as _mybir
    from concourse.bass_utils import run_bass_kernel_spmd as _run

    nc = _bacc.Bacc("TRN2", target_bir_lowering=False, num_devices=1)
    arrays, args = {}, []
    for name in _INS:
        a = _np.ascontiguousarray(inputs[name])
        arrays[f"in_{name}"] = a
        args.append(nc.dram_tensor(f"in_{name}", a.shape, _mybir.dt.from_np(a.dtype), kind="ExternalInput").ap())
    args.append(nc.dram_tensor("out_x", (N, D), F32, kind="ExternalOutput").ap())
    graph_layers(nc, *args)
    r = _run(nc, [arrays], core_ids=[0])
    return r.results[0]["out_x"]
```
